# Optimizing a Trainium2 kernel written in Bass

```python
import numpy as np
import jax
import jax.numpy as jnp

def _softmax(x, axis=-1):
    return jax.nn.softmax(x, axis=axis)

def _gelu(x):
    return jax.nn.gelu(x, approximate=True)

def _silu(x):
    return jax.nn.silu(x)

def _sigmoid(x):
    return jax.nn.sigmoid(x)

def _layernorm(x, axis=-1, eps=1e-05):
    m = jnp.mean(x, axis=axis, keepdims=True)
    v = jnp.var(x, axis=axis, keepdims=True)
    return (x - m) / jnp.sqrt(v + eps)

def _scatter_add(tgt, idx, src, axis=0):
    return tgt.at[idx].add(src)

def _segment_sum(src, seg, n):
    return jax.ops.segment_sum(src, seg, n)
kernel_name = 'mk_flamingo_gated_d2_seqx_r8_8f7188'

def setup_inputs(seed: int=0):
    np.random.seed(seed)
    _w = jnp.asarray

    def _rec_inputs():
        import jax
        import jax.numpy as jnp
        _rk = jax.random.key(seed)
        x = 7.22e-05 + 1 * jax.random.normal(jax.random.fold_in(_rk, 1), (16, 128, 128), jnp.float32)
        _lenS = 128 - jax.random.randint(jax.random.fold_in(_rk, 7), (16,), 0, max(1, 128 // 4) + 1, jnp.int32)
        _lenS2 = 120 - jax.random.randint(jax.random.fold_in(_rk, 8), (16,), 0, max(1, 120 // 4) + 1, jnp.int32)
        _ctx_1024P = jax.random.normal(jax.random.fold_in(_rk, 11), (16, 16, 128), jnp.float32)
        _ctx_1024c = jax.random.dirichlet(jax.random.fold_in(_rk, 511), 0.3 * jnp.ones((16,), jnp.float32), (16, 120))
        _ctx_1024t = jnp.einsum('bsk,bkd->bsd', _ctx_1024c, _ctx_1024P)
        _ctx_1024t = _ctx_1024t * jax.lax.rsqrt(jnp.mean(jnp.square(_ctx_1024t)) + 1e-12) * 0.953939
        ctx_1024 = 4.13588e-05 + 0.999923 * (_ctx_1024t + 0.3 * jax.random.normal(jax.random.fold_in(_rk, 611), (16, 120, 128), jnp.float32))
        _validS = jnp.arange(128)[None, :] < _lenS[:, None]
        _validS2 = jnp.arange(120)[None, :] < _lenS2[:, None]
        _causal = jnp.tril(jnp.ones((128, 128), dtype=bool))
        mask_Bx1xSxS2_bk1 = jnp.broadcast_to(_validS2[:, None, None, :], (16, 1, 128, 120))
        _g = jax.random.normal(jax.random.fold_in(_rk, 9001), (2, 2), jnp.float32)
        _g = jnp.sign(_g) * jnp.maximum(jnp.abs(_g), 1.0) + (_g == 0) * 1.0
        g_xattn = _g[0]
        g_ffn = _g[1]
        return (x, ctx_1024, mask_Bx1xSxS2_bk1, g_xattn, g_ffn)
    x, ctx_1024, mask_Bx1xSxS2_bk1, g_xattn, g_ffn = _rec_inputs()

    def _L0_xattn_setup():
        import jax, jax.numpy as jnp
        import numpy as np
        B, S, D, H = (4, 256, 128, 16)
        HD = D // H
        key = jax.random.key(seed)
        ks = jax.random.split(key, 12)
        scale = 1.0 / np.sqrt(D)
        inp = {'queries': jax.random.normal(ks[0], (B, S, D), jnp.float32), 'keys': jax.random.normal(ks[1], (B, S, D), jnp.float32), 'values': jax.random.normal(ks[2], (B, S, D), jnp.float32), 'mask': jax.random.randint(ks[3], (B, 1, S, S), 0, 2).astype(bool), 'Wq': jax.random.normal(ks[4], (D, D), jnp.float32) * scale, 'bq': jnp.zeros((D,), jnp.float32), 'Wk': jax.random.normal(ks[5], (D, D), jnp.float32) * scale, 'bk': jnp.zeros((D,), jnp.float32), 'Wv': jax.random.normal(ks[6], (D, D), jnp.float32) * scale, 'bv': jnp.zeros((D,), jnp.float32), 'Wo': jax.random.normal(ks[7], (D, D), jnp.float32) * scale, 'bo': jnp.zeros((D,), jnp.float32)}
        return inp
    _L0_xattn_all = _L0_xattn_setup()
    _L0_xattn_in = {k: v for k, v in _L0_xattn_all.items() if k in ('Wq', 'bq', 'Wk', 'bk', 'Wv', 'bv', 'Wo', 'bo')}
    del _L0_xattn_all

    def _L0_ffn_setup():
        import jax, jax.numpy as jnp
        import numpy as np
        B, S, D, E, H, K = (4, 256, 128, 8, 64, 2)
        key = jax.random.key(seed)
        ks = jax.random.split(key, 11)
        sc = 0.02
        return {'x': jax.random.normal(ks[0], (B, S, D), dtype=jnp.float32), 'gate_W': jax.random.normal(ks[1], (D, E), dtype=jnp.float32) * sc, 'W1': jax.random.normal(ks[2], (E, D, H), dtype=jnp.float32) * sc, 'b1': jnp.zeros((E, H), dtype=jnp.float32), 'W2': jax.random.normal(ks[3], (E, H, D), dtype=jnp.float32) * sc, 'b2': jnp.zeros((E, D), dtype=jnp.float32), 'Ws1': jax.random.normal(ks[4], (D, H), dtype=jnp.float32) * sc, 'bs1': jnp.zeros((H,), dtype=jnp.float32), 'Ws2': jax.random.normal(ks[5], (H, D), dtype=jnp.float32) * sc, 'bs2': jnp.zeros((D,), dtype=jnp.float32), 'route_scale': jnp.ones((), dtype=jnp.float32)}
    _L0_ffn_all = _L0_ffn_setup()
    _L0_ffn_in = {k: v for k, v in _L0_ffn_all.items() if k in ('gate_W', 'W1', 'b1', 'W2', 'b2', 'Ws1', 'bs1', 'Ws2', 'bs2', 'route_scale')}
    del _L0_ffn_all

    def _L1_xattn_setup():
        import jax, jax.numpy as jnp
        import numpy as np
        MODEL_DIM = 128
        HEADS = 16
        HEAD_DIM = MODEL_DIM // HEADS
        OUT_DIM = 128
        B, S = (2, 256)

        def _split_heads(x):
            b, s, _ = x.shape
            return x.reshape(b, s, HEADS, HEAD_DIM).transpose(0, 2, 1, 3)
        key = jax.random.key(seed)
        ks = jax.random.split(key, 10)
        scale = 1.0 / np.sqrt(MODEL_DIM)
        return {'query': jax.random.normal(ks[0], (B, S, MODEL_DIM), dtype=jnp.float32), 'bank': jax.random.normal(ks[1], (B, S, MODEL_DIM), dtype=jnp.float32), 'Wq': jax.random.normal(ks[2], (MODEL_DIM, MODEL_DIM), dtype=jnp.float32) * scale, 'bq': jnp.zeros((MODEL_DIM,), dtype=jnp.float32), 'Wk': jax.random.normal(ks[3], (MODEL_DIM, MODEL_DIM), dtype=jnp.float32) * scale, 'bk': jnp.zeros((MODEL_DIM,), dtype=jnp.float32), 'Wv': jax.random.normal(ks[4], (MODEL_DIM, MODEL_DIM), dtype=jnp.float32) * scale, 'bv': jnp.zeros((MODEL_DIM,), dtype=jnp.float32), 'Wo': jax.random.normal(ks[5], (OUT_DIM, MODEL_DIM), dtype=jnp.float32) * scale, 'bo': jnp.zeros((OUT_DIM,), dtype=jnp.float32)}
    _L1_xattn_all = _L1_xattn_setup()
    _L1_xattn_in = {k: v for k, v in _L1_xattn_all.items() if k in ('Wq', 'bq', 'Wk', 'bk', 'Wv', 'bv', 'Wo', 'bo')}
    del _L1_xattn_all

    def _L1_ffn_setup():
        import jax, jax.numpy as jnp
        import numpy as np
        DIM = 128

        def _reference_tuple_inner(x, W_r, W_k, W_v, mu_r, mu_k):
            B, T, C = x.shape
            x_prev = jnp.concatenate([jnp.zeros((B, 1, C), x.dtype), x[:, :-1, :]], axis=1)
            xr = mu_r * x + (1.0 - mu_r) * x_prev
            xk = mu_k * x + (1.0 - mu_k) * x_prev
            r = jax.nn.sigmoid(jnp.einsum('btc,dc->btd', xr, W_r))
            k = jnp.einsum('btc,dc->btd', xk, W_k)
            k_act = jnp.square(jax.nn.relu(k))
            out = r * jnp.einsum('btc,dc->btd', k_act, W_v)
            new_state = x[:, -1, :]
            return (out, new_state)
        key = jax.random.key(seed)
        ks = jax.random.split(key, 6)
        B, T, C = (8, 256, DIM)
        x = jax.random.normal(ks[0], (B, T, C), dtype=jnp.float32)
        s = 1.0 / np.sqrt(C)
        W_r = jax.random.uniform(ks[1], (C, C), jnp.float32, -s, s)
        W_k = jax.random.uniform(ks[2], (C, C), jnp.float32, -s, s)
        W_v = jax.random.uniform(ks[3], (C, C), jnp.float32, -s, s)
        mu_r = jax.random.uniform(ks[4], (C,), jnp.float32)
        mu_k = jax.random.uniform(ks[5], (C,), jnp.float32)
        return {'x': x, 'W_r': W_r, 'W_k': W_k, 'W_v': W_v, 'mu_r': mu_r, 'mu_k': mu_k}
    _L1_ffn_all = _L1_ffn_setup()
    _L1_ffn_in = {k: v for k, v in _L1_ffn_all.items() if k in ('W_r', 'W_k', 'W_v', 'mu_r', 'mu_k')}
    del _L1_ffn_all
    return {'x': x, 'ctx_1024': ctx_1024, 'mask_Bx1xSxS2_bk1': mask_Bx1xSxS2_bk1, 'g_xattn': g_xattn, 'g_ffn': g_ffn, 'L0_xattn_Wq': _L0_xattn_in['Wq'], 'L0_xattn_bq': _L0_xattn_in['bq'], 'L0_xattn_Wk': _L0_xattn_in['Wk'], 'L0_xattn_bk': _L0_xattn_in['bk'], 'L0_xattn_Wv': _L0_xattn_in['Wv'], 'L0_xattn_bv': _L0_xattn_in['bv'], 'L0_xattn_Wo': _L0_xattn_in['Wo'], 'L0_xattn_bo': _L0_xattn_in['bo'], 'L0_ffn_gate_W': _L0_ffn_in['gate_W'], 'L0_ffn_W1': _L0_ffn_in['W1'], 'L0_ffn_b1': _L0_ffn_in['b1'], 'L0_ffn_W2': _L0_ffn_in['W2'], 'L0_ffn_b2': _L0_ffn_in['b2'], 'L0_ffn_Ws1': _L0_ffn_in['Ws1'], 'L0_ffn_bs1': _L0_ffn_in['bs1'], 'L0_ffn_Ws2': _L0_ffn_in['Ws2'], 'L0_ffn_bs2': _L0_ffn_in['bs2'], 'L0_ffn_route_scale': _L0_ffn_in['route_scale'], 'L1_xattn_Wq': _L1_xattn_in['Wq'], 'L1_xattn_bq': _L1_xattn_in['bq'], 'L1_xattn_Wk': _L1_xattn_in['Wk'], 'L1_xattn_bk': _L1_xattn_in['bk'], 'L1_xattn_Wv': _L1_xattn_in['Wv'], 'L1_xattn_bv': _L1_xattn_in['bv'], 'L1_xattn_Wo': _L1_xattn_in['Wo'], 'L1_xattn_bo': _L1_xattn_in['bo'], 'L1_ffn_W_r': _L1_ffn_in['W_r'], 'L1_ffn_W_k': _L1_ffn_in['W_k'], 'L1_ffn_W_v': _L1_ffn_in['W_v'], 'L1_ffn_mu_r': _L1_ffn_in['mu_r'], 'L1_ffn_mu_k': _L1_ffn_in['mu_k']}

def reference(x, ctx_1024, mask_Bx1xSxS2_bk1, g_xattn, g_ffn, L0_xattn_Wq, L0_xattn_bq, L0_xattn_Wk, L0_xattn_bk, L0_xattn_Wv, L0_xattn_bv, L0_xattn_Wo, L0_xattn_bo, L0_ffn_gate_W, L0_ffn_W1, L0_ffn_b1, L0_ffn_W2, L0_ffn_b2, L0_ffn_Ws1, L0_ffn_bs1, L0_ffn_Ws2, L0_ffn_bs2, L0_ffn_route_scale, L1_xattn_Wq, L1_xattn_bq, L1_xattn_Wk, L1_xattn_bk, L1_xattn_Wv, L1_xattn_bv, L1_xattn_Wo, L1_xattn_bo, L1_ffn_W_r, L1_ffn_W_k, L1_ffn_W_v, L1_ffn_mu_r, L1_ffn_mu_k):
    import jax
    import jax.numpy as jnp

    def _L0_xattn_ref(queries, keys, values, mask, Wq, bq, Wk, bk, Wv, bv, Wo, bo):
        import jax, jax.numpy as jnp
        import numpy as np
        B, S, D, H = (4, 256, 128, 16)
        HD = D // H
        b, sq, d = queries.shape

        def split_heads(x):
            return x.reshape(b, x.shape[1], H, HD).transpose(0, 2, 1, 3)
        q = split_heads(queries @ Wq + bq)
        k = split_heads(keys @ Wk + bk)
        v = split_heads(values @ Wv + bv)
        scores = jnp.einsum('bhqd,bhkd->bhqk', q, k) / jnp.sqrt(jnp.float32(HD))
        scores = jnp.where(mask, jnp.float32(-1000000000000000.0), scores)
        attn = jax.nn.softmax(scores, axis=-1)
        ctx = jnp.einsum('bhqk,bhkd->bhqd', attn, v)
        ctx = ctx.transpose(0, 2, 1, 3).reshape(b, sq, d)
        return ctx @ Wo + bo

    def _L0_ffn_ref(x, gate_W, W1, b1, W2, b2, Ws1, bs1, Ws2, bs2, route_scale):
        import jax, jax.numpy as jnp
        import numpy as np
        B, S, D, E, H, K = (4, 256, 128, 8, 64, 2)
        scores = jax.nn.sigmoid(x @ gate_W) * route_scale
        topk_scores, topk_idx = jax.lax.top_k(scores, K)
        topk_w = topk_scores / topk_scores.sum(-1, keepdims=True)
        onehot = jax.nn.one_hot(topk_idx, E, dtype=x.dtype)
        gate_full = jnp.einsum('bsk,bske->bse', topk_w, onehot)
        h = jax.nn.gelu(jnp.einsum('bsd,edh->bseh', x, W1) + b1, approximate=False)
        y = jnp.einsum('bseh,ehd->bsed', h, W2) + b2
        expert_out = jnp.einsum('bse,bsed->bsd', gate_full, y)
        shared = jax.nn.gelu(x @ Ws1 + bs1, approximate=False) @ Ws2 + bs2
        return expert_out + shared

    def _L1_xattn_ref(query, bank, Wq, bq, Wk, bk, Wv, bv, Wo, bo):
        import jax, jax.numpy as jnp
        import numpy as np
        MODEL_DIM = 128
        HEADS = 16
        HEAD_DIM = MODEL_DIM // HEADS
        OUT_DIM = 128
        B, S = (2, 256)

        def _split_heads(x):
            b, s, _ = x.shape
            return x.reshape(b, s, HEADS, HEAD_DIM).transpose(0, 2, 1, 3)
        q = _split_heads(query @ Wq.T + bq)
        k = _split_heads(bank @ Wk.T + bk)
        v = _split_heads(bank @ Wv.T + bv)
        score_scale = jnp.sqrt(jnp.float32(HEAD_DIM))
        scores = jnp.einsum('bhqd,bhkd->bhqk', q / score_scale, k)
        attn = jax.nn.softmax(scores, axis=-1)
        ctx = jnp.einsum('bhqk,bhkd->bhqd', attn, v)
        b, h, sq, hd = ctx.shape
        ctx = ctx.transpose(0, 2, 1, 3).reshape(b, sq, MODEL_DIM)
        return ctx @ Wo.T + bo

    def _L1_ffn_ref(x, W_r, W_k, W_v, mu_r, mu_k):
        import jax, jax.numpy as jnp
        import numpy as np
        DIM = 128

        def _reference_tuple_inner(x, W_r, W_k, W_v, mu_r, mu_k):
            B, T, C = x.shape
            x_prev = jnp.concatenate([jnp.zeros((B, 1, C), x.dtype), x[:, :-1, :]], axis=1)
            xr = mu_r * x + (1.0 - mu_r) * x_prev
            xk = mu_k * x + (1.0 - mu_k) * x_prev
            r = jax.nn.sigmoid(jnp.einsum('btc,dc->btd', xr, W_r))
            k = jnp.einsum('btc,dc->btd', xk, W_k)
            k_act = jnp.square(jax.nn.relu(k))
            out = r * jnp.einsum('btc,dc->btd', k_act, W_v)
            new_state = x[:, -1, :]
            return (out, new_state)
        return _reference_tuple_inner(x, W_r, W_k, W_v, mu_r, mu_k)[0]
    x = x + jnp.tanh(g_xattn[0]) * _L0_xattn_ref(_layernorm(x, axis=-1), ctx_1024, ctx_1024, mask_Bx1xSxS2_bk1, L0_xattn_Wq, L0_xattn_bq, L0_xattn_Wk, L0_xattn_bk, L0_xattn_Wv, L0_xattn_bv, L0_xattn_Wo, L0_xattn_bo)
    x = x + jnp.tanh(g_ffn[0]) * _L0_ffn_ref(_layernorm(x, axis=-1), L0_ffn_gate_W, L0_ffn_W1, L0_ffn_b1, L0_ffn_W2, L0_ffn_b2, L0_ffn_Ws1, L0_ffn_bs1, L0_ffn_Ws2, L0_ffn_bs2, L0_ffn_route_scale)
    x = x + jnp.tanh(g_xattn[1]) * _L1_xattn_ref(_layernorm(x, axis=-1), ctx_1024, L1_xattn_Wq, L1_xattn_bq, L1_xattn_Wk, L1_xattn_bk, L1_xattn_Wv, L1_xattn_bv, L1_xattn_Wo, L1_xattn_bo)
    x = x + jnp.tanh(g_ffn[1]) * _L1_ffn_ref(_layernorm(x, axis=-1), L1_ffn_W_r, L1_ffn_W_k, L1_ffn_W_v, L1_ffn_mu_r, L1_ffn_mu_k)
    return x

_drawn_inputs = setup_inputs


def setup_inputs(seed=0):
    import zlib

    import numpy as np

    out = dict(_drawn_inputs(seed))
    spreads = {'g_ffn': (-1.0, 0.6),
     'L0_xattn_bq': (0.0, 0.365),
     'L0_xattn_bk': (0.0, 0.8),
     'L0_xattn_bv': (0.0, 0.1),
     'L0_xattn_bo': (0.0, 0.1),
     'L0_ffn_b1': (0.0, 0.8),
     'L0_ffn_b2': (0.0, 0.1),
     'L0_ffn_bs1': (0.0, 0.8),
     'L0_ffn_bs2': (0.0, 0.1),
     'L1_xattn_bq': (0.0, 0.441),
     'L1_xattn_bk': (0.0, 0.8),
     'L1_xattn_bv': (0.0, 0.1),
     'L1_xattn_bo': (0.0, 0.1)}
    factors = {'L0_ffn_W1': 6.899,
     'L0_ffn_W2': 6.217,
     'L0_ffn_Ws1': 4.812,
     'L0_ffn_Ws2': 4.361,
     'L1_ffn_W_r': 3.769,
     'L1_ffn_mu_r': 8.0}
    for name, (base, spread) in spreads.items():
        noise = np.random.default_rng([zlib.crc32(name.encode()), seed]).standard_normal(out[name].shape)
        drawn = base * np.exp(spread * noise) if base else spread * noise
        out[name] = jnp.asarray(drawn.astype(out[name].dtype))
    for name, factor in factors.items():
        out[name] = (out[name] * factor).astype(out[name].dtype)
    return out
```

```python
import concourse.bass as bass
from concourse import mybir
from contextlib import ExitStack

F32 = mybir.dt.float32
BF16 = mybir.dt.bfloat16
FP16 = mybir.dt.float16
U8 = mybir.dt.uint8
ALU = mybir.AluOpType
ACT = mybir.ActivationFunctionType
AX = mybir.AxisListType

B, S, SK, D = 16, 128, 120, 128
H, HD = 16, 8
E, HID = 8, 64
PARTS = 3
STACK = PARTS * PARTS * HD
ROWS = STACK + PARTS
VC = PARTS * HD + 1
NG, GB = 4, 4
GT, GK = GB * S, GB * SK
UNITS, UH = 4, 4
LAYERS = 2
MASKED = -float(2 ** 50)
EPS = 1e-5
SCALE = float(HD) ** -0.5
LIFT = 6.931471805599453
NBLK = E * HID // 128


def gated_blocks(nc, x, ctxT, mask, wts, w2sh, bcols, brows, gates, ident, identh, sel, rank, onesrows, out):
    ctx = ExitStack()
    with ctx:
        def sb(name, shape, dt=F32):
            return ctx.enter_context(nc.sbuf_tensor(name, shape, dt))

        def sem(name):
            return ctx.enter_context(nc.semaphore(name))

        X = sb("X", [S, B, D])
        CT = sb("CT", [D, B * SK])
        WT = sb("WT", [128, 21 * 128])
        W2S = sb("W2S", [HID + E + 1, 128])
        BC = sb("BC", [128, 11])
        BR = sb("BR", [128, 4, 128])
        GA = sb("GA", [128, 5])
        TG = sb("TG", [128, 4])
        IDF = sb("IDF", [128, 128])
        IDH = sb("IDH", [128, 128], BF16)
        SEL = sb("SEL", [PARTS * E, NBLK * 128], BF16)
        RANK = sb("RANK", [128, GB, E])
        MU8 = sb("MU8", [S, B, SK], U8)
        MB = sb("MB", [S, B, SK], BF16)
        bqs = sb("bqs", [128, LAYERS])
        tgbo = sb("tgbo", [128, LAYERS, 128])
        mu1 = sb("mu1", [128, 2])
        epsT = sb("epsT", [128, GB])
        powT = sb("powT", [128, GB])
        st6 = sb("st6", [S, GB, 6])
        mv = sb("mv", [S, GB, 2])
        ve = sb("ve", [S, GB])
        rstd = sb("rstd", [S, GB])
        xn = sb("xn", [S, GB, D])
        xnT = sb("xnT", [D, GT])
        qf = sb("qf", [128, GT])
        qr = sb("qr", [128, GT])
        qp = sb("qp", [128, PARTS, GT], BF16)
        kf = sb("kf", [128, GK])
        kr = sb("kr", [128, GK])
        kp = sb("kp", [128, PARTS, GK], BF16)
        vf = sb("vf", [SK, GB, D])
        vr = sb("vr", [SK, GB, D])
        QS = [sb(f"QS{i}", [ROWS, H, GT], BF16) for i in range(2)]
        KS = [sb(f"KS{i}", [ROWS, H, GK], BF16) for i in range(2)]
        VS = [sb(f"VS{i}", [SK, GB, H, VC], BF16) for i in range(2)]
        nmx = [sb(f"nmx{i}", [S, H]) for i in range(2)]
        nmr = sb("nmr", [S, H])
        nmp = [sb(f"nmp{i}", [S, PARTS, H], BF16) for i in range(2)]
        nmT = [sb(f"nmT{i}", [PARTS * H, S], BF16) for i in range(2)]
        P32 = [sb(f"P32{i}", [SK, H, S]) for i in range(2)]
        P1 = [sb(f"P1{i}", [SK, H, S], FP16) for i in range(2)]
        P2 = [sb(f"P2{i}", [SK, H, S], FP16) for i in range(2)]
        num = sb("num", [S, H, HD])
        rec = sb("rec", [S, H])
        cn = [sb(f"cn{i}", [S, D]) for i in range(2)]
        cT = [sb(f"cT{i}", [D, S]) for i in range(2)]
        hT = sb("hT", [128, 2, GT])
        hs = sb("hs", [128, NBLK, GT])
        h5 = sb("h5", [HID + E + 1, GT])
        sc = sb("sc", [S, GB, E])
        m1 = sb("m1", [S, GB])
        m2 = sb("m2", [S, GB])
        eq = sb("eq", [S, GB, E])
        mw = sb("mw", [S, GB])
        oh1 = sb("oh1", [S, GB, E])
        oh2 = sb("oh2", [S, GB, E])
        s2 = sb("s2", [S, GB, E])
        den = sb("den", [S, GB])
        gw = sb("gw", [S, GB, 2])
        gr = sb("gr", [S, GB, E])
        gp = sb("gp", [S, GB, PARTS, E], BF16)
        gx = sb("gx", [S, GB, HID + E + 1])
        gpT = sb("gpT", [PARTS * E, GT], BF16)
        xsh = sb("xsh", [D, GB, S + 1])
        tr_ = sb("tr_", [D, GB, S])
        tk_ = sb("tk_", [D, GB, S])
        xr = sb("xr", [D, GB, S])
        xk = sb("xk", [D, GB, S])
        rs = sb("rs", [S, GB, D])
        kre = sb("kre", [D, GT])
        ksq = sb("ksq", [D, GT])
        yv = sb("yv", [S, GB, D])

        bank = [ctx.enter_context(nc.psum_tensor(f"bank{i}", [128, 512], F32)) for i in range(8)]
        qparts = nc.dram_tensor("qparts", [2, 128, PARTS, GT], BF16).ap()
        kparts = nc.dram_tensor("kparts", [2, 128, PARTS, GK], BF16).ap()

        def W(i, n=128):
            return WT[:, i * 128:i * 128 + n]

        WQ, WK, WV, WO = [0, 4], [1, 5], [2, 6], [3, 7]
        W1, WSH, WGATE, W2, WR, WKK, WVV = 8, 12, 13, 14, 18, 19, 20

        x_in = [sem(f"x_in{i}") for i in range(NG)]
        w_in = sem("w_in"); w_in2 = sem("w_in2"); c_in = sem("c_in"); m_in = sem("m_in")
        ones_in = sem("ones_in")
        tg_ok = sem("tg_ok"); consts_ok = sem("consts_ok"); mb_ok = sem("mb_ok")
        pool_c = sem("pool_c")
        dve_c = sem("dve_c")
        act_c = sem("act_c")
        ln_var = sem("ln_var"); ln_rstd = sem("ln_rstd"); xn_ok = sem("xn_ok"); xb_ok = sem("xb_ok")
        xt_done = sem("xt_done"); xt_evac = sem("xt_evac")
        q_done = sem("q_done"); q_evac = sem("q_evac"); q_split = sem("q_split")
        q_st = sem("q_st"); q_ld = [sem("q_ld0"), sem("q_ld1")]
        k_done = sem("k_done"); k_evac = sem("k_evac"); k_split = sem("k_split")
        k_st = sem("k_st"); k_ld = [sem("k_ld0"), sem("k_ld1")]
        v_done = sem("v_done"); v_f = sem("v_f"); v_1 = sem("v_1"); v_r = sem("v_r"); v_2 = sem("v_2"); v_3 = sem("v_3")
        qm_done = sem("qm_done"); max_done = sem("max_done"); nm_ok = sem("nm_ok")
        nt_done = sem("nt_done"); nt_evac = sem("nt_evac"); m_ld = [sem("m_ld0"), sem("m_ld1")]
        km_done = sem("km_done"); exp_done = sem("exp_done"); p2_done = sem("p2_done")
        pv_done = sem("pv_done"); cn_ok = sem("cn_ok"); ct_done = sem("ct_done"); ct_evac = sem("ct_evac")
        op_done = sem("op_done"); xa_ok = sem("xa_ok")
        lg_done = sem("lg_done"); sg_ok = sem("sg_ok"); g_ok = sem("g_ok"); gt_done = sem("gt_done"); gt_evac = sem("gt_evac")
        h_done = sem("h_done"); h_act = sem("h_act"); gb_done = sem("gb_done"); hs_ok = sem("hs_ok")
        y_done = sem("y_done"); xf_ok = sem("xf_ok")
        xs_evac = sem("xs_evac"); mix_t = sem("mix_t"); xr_ok = sem("xr_ok"); xk_ok = sem("xk_ok")
        r_done = sem("r_done"); r_act = sem("r_act"); kk_done = sem("kk_done"); kr_ok = sem("kr_ok"); ks_ok = sem("ks_ok")
        vv_done = sem("vv_done"); y_ok = sem("y_ok"); xo_ok = sem("xo_ok"); o_out = sem("o_out")

        block = ctx.enter_context(nc.Block())

        def bseq(Bi):
            return Bi % B, Bi // GB, Bi % GB

        NB = LAYERS * B

        def after_v(s, G):
            return 1 <= s // GB <= NG and s % GB == 0 and G - 1 < LAYERS * NG

        def ln_no(phase, g):
            return phase * NG + g

        @block.sync
        def _(sp):
            for g in range(NG):
                sp.dma_start(X[:, GB * g:GB * g + GB, :], x[GB * g:GB * g + GB, :, :].rearrange("b s d -> s b d")).then_inc(x_in[g], 16)
                if g == 0:
                    sp.dma_start(CT[:, :], ctxT).then_inc(c_in, 16)
                    sp.dma_start(WT[:, 0:4 * 128], wts[:, 0:4 * 128]).then_inc(w_in, 16)
                    sp.dma_start(BC[:, :], bcols).then_inc(w_in, 16)
                    sp.dma_start(IDF[:, :], ident).then_inc(w_in, 16)
                    sp.dma_start(GA[:, :], gates.broadcast_to([128, 5])).then_inc(w_in, 16)
                    sp.dma_start(BR[:, :, :], brows.broadcast_to([128, 4, 128])).then_inc(w_in, 16)
                    sp.dma_start(IDH[:, :], identh).then_inc(w_in, 16)
                    sp.dma_start(MU8[:, :, :], mask.rearrange("b s k -> s b k")).then_inc(m_in, 16)
                    for i in range(2):
                        sp.dma_start(KS[i][STACK:ROWS, :, :], onesrows).then_inc(ones_in, 16)
            sp.dma_start(WT[:, 4 * 128:], wts[:, 4 * 128:]).then_inc(w_in2, 16)
            sp.dma_start(W2S[:, :], w2sh).then_inc(w_in2, 16)
            sp.dma_start(SEL[:, :], sel).then_inc(w_in2, 16)
            sp.dma_start(RANK[:, :, :], rank).then_inc(w_in2, 16)

            def k_store(G):
                sp.wait_ge(k_split, G + 1)
                if G >= 2:
                    sp.wait_ge(k_ld[G % 2], 144 * (G // 2))
                sp.dma_start(kparts[G % 2], kp[:, :, :]).then_inc(k_st, 16)

            def k_load(G):
                sp.wait_ge(k_st, 16 * (G + 1))
                if G >= 2:
                    sp.wait_ge(km_done, (G - 1) * GB * UNITS)
                src = kparts[G % 2].rearrange("(h d) c t -> c d h t", d=HD)
                for a in range(PARTS):
                    for c in range(PARTS):
                        r = (a * PARTS + c) * HD
                        sp.dma_start(KS[G % 2][r:r + HD, :, :], src[c]).then_inc(k_ld[G % 2], 16)

            def q_store(G):
                sp.wait_ge(q_split, G + 1)
                if G >= 2:
                    sp.wait_ge(q_ld[G % 2], 144 * (G // 2))
                sp.dma_start(qparts[G % 2], qp[:, :, :]).then_inc(q_st, 16)

            def q_load(G):
                sp.wait_ge(q_st, 16 * (G + 1))
                if G >= 2:
                    sp.wait_ge(km_done, (G - 1) * GB * UNITS)
                src = qparts[G % 2].rearrange("(h d) a t -> a d h t", d=HD)
                for a in range(PARTS):
                    for c in range(PARTS):
                        r = (a * PARTS + c) * HD
                        sp.dma_start(QS[G % 2][r:r + HD, :, :], src[a]).then_inc(q_ld[G % 2], 16)

            def max_rows(Bi):
                b, G, k = bseq(Bi)
                sp.wait_ge(nt_evac, Bi + 1)
                if G >= 2 and k == 0:
                    sp.wait_ge(km_done, (G - 1) * GB * UNITS)
                for p in range(PARTS):
                    sp.dma_start(QS[G % 2][STACK + p:STACK + p + 1, :, k * S:(k + 1) * S],
                                 nmT[Bi % 2][p * H:(p + 1) * H, :]).then_inc(m_ld[Bi % 2], 16)

            def prep_slot(G, k):
                if k == 1:
                    k_store(G)
                if k == 2:
                    k_load(G)
                    if G != NG:
                        q_store(G)
                        q_load(G)

            k_store(0); k_load(0); q_store(0); q_load(0)
            for L in range(LAYERS):
                for s in range(B + 1):
                    if s >= 1:
                        max_rows(L * B + s - 1)
                    if s < B:
                        G = L * NG + s // GB + 1
                        if G < LAYERS * NG:
                            prep_slot(G, s % GB)
                if L == 0:
                    q_store(NG); q_load(NG)
            for g in range(NG):
                sp.wait_ge(xo_ok, g + 1)
                sp.dma_start(out[GB * g:GB * g + GB, :, :].rearrange("b s d -> s b d"), X[:, GB * g:GB * g + GB, :]).then_inc(o_out, 16)
            sp.wait_ge(o_out, 16 * NG)

        @block.gpsimd
        def _(po):
            po.memset(epsT[:, :], EPS).then_inc(pool_c, 1)
            po.memset(powT[:, :], -0.5).then_inc(pool_c, 1)
            for i in range(2):
                po.memset(VS[i][:, :, :, PARTS * HD:VC], 1.0).then_inc(pool_c, 1)
            po.memset(gx[:, :, :], 0.0).then_inc(pool_c, 1)
            po.memset(xsh[:, :, 0:1], 0.0).then_inc(pool_c, 1)
            po.wait_ge(pool_c, 6)
            po.memset(gx[:, :, HID + E:], 1.0).then_inc(pool_c, 1)

            def ln_rstd_(n):
                po.wait_ge(ln_var, n + 1)
                po.tensor_tensor(ve[:, :], mv[:, :, 1], epsT[:, :], ALU.add).then_inc(ln_rstd, 1)
                po.wait_ge(ln_rstd, 2 * n + 1)
                po.tensor_tensor(rstd[:, :], ve[:, :], powT[:, :], ALU.pow).then_inc(ln_rstd, 1)

            def bias_on_x(G):
                L, g = G // NG, G % NG
                po.wait_ge(xn_ok, ln_no(2 * L, g) + 1)
                if G == 0:
                    po.wait_ge(consts_ok, 1)
                xg = X[:, GB * g:GB * g + GB, :]
                po.tensor_tensor(xg, xg, tgbo[:, L, :].unsqueeze(1).broadcast_to([S, GB, D]), ALU.add).then_inc(xb_ok, 1)

            def v_rest(G, part):
                if part == 2:
                    po.wait_ge(v_1, G + 1)
                    po.tensor_tensor(vr[:, :, :], vf[:, :, :], VS4(G, 0), ALU.subtract).then_inc(v_r, 1)
                else:
                    po.wait_ge(v_2, G + 1)
                    po.wait_ge(v_r, G + 1)
                    vrr = vr[:, :, :].rearrange("p b (h d) -> p b h d", d=HD)
                    po.tensor_tensor(VS[G % 2][:, :, :, 2 * HD:3 * HD], vrr, VS[G % 2][:, :, :, HD:2 * HD], ALU.subtract).then_inc(v_3, 1)

            def VS4(G, p):
                return VS[G % 2][:, :, :, p * HD:(p + 1) * HD].rearrange("p b h d -> p b h d")

            def p_low(Bi, half):
                po.wait_ge(exp_done, Bi * UNITS + 2 * half + 2)
                if Bi >= 2:
                    po.wait_ge(pv_done, Bi - 1)
                hh = slice(8 * half, 8 * half + 8)
                po.tensor_tensor(P2[Bi % 2][:, hh, :], P32[Bi % 2][:, hh, :], P1[Bi % 2][:, hh, :], ALU.subtract).then_inc(p2_done, 1)

            def prep(G, stage):
                if stage == "ln":
                    ln_rstd_(ln_no(2 * (G // NG), G % NG))
                if stage == "bias":
                    bias_on_x(G)
                if stage == "v2":
                    v_rest(G, 2)
                if stage == "v3":
                    v_rest(G, 3)

            prep(0, "v2"); prep(0, "v3"); prep(0, "ln"); prep(0, "bias")
            for L in range(LAYERS):
                for s in range(B + 3):
                    G = L * NG + s // GB + 1
                    live = s < B and G < LAYERS * NG
                    k = s % GB
                    if live and k == 0 and G != NG:
                        prep(G, "ln")
                    if live and k == 1 and G != NG:
                        prep(G, "bias")
                    if 2 <= s < B + 2:
                        p_low(L * B + s - 2, 0)
                    if 2 <= s < B + 2:
                        p_low(L * B + s - 2, 1)
                    if live and k == 3:
                        prep(G, "v2")
                    if after_v(s, G):
                        prep(G - 1, "v3")
                if L == 0:
                    for g in range(NG):
                        ln_rstd_(ln_no(1, g))
                    prep(NG, "ln")
                    prep(NG, "bias")
                else:
                    for g in range(NG):
                        ln_rstd_(ln_no(3, g))

        @block.vector
        def _(v):
            n_chain = [0]

            def link(ins):
                n_chain[0] += 1
                ins.then_inc(dve_c, 1)
                v.wait_ge(dve_c, n_chain[0])

            def ln(phase, g):
                n = ln_no(phase, g)
                if phase == 0:
                    v.wait_ge(x_in[g], 16)
                if n >= 1:
                    v.wait_ge(ln_rstd, 2 * n)
                for i in range(GB):
                    nc.vector.bn_stats(st6[:, i, :], X[:, GB * g + i, :]).then_inc(dve_c, 1)
                n_chain[0] += GB
                v.wait_ge(dve_c, n_chain[0])
                for i in range(GB):
                    ins = nc.vector.bn_aggr(mv[:, i, :], st6[:, i, :])
                    if i < GB - 1:
                        ins.then_inc(dve_c, 1)
                n_chain[0] += GB - 1
                ins.then_inc(ln_var, 1)

            def ln_apply(phase, g):
                n = ln_no(phase, g)
                v.wait_ge(ln_rstd, 2 * n + 2)
                v.wait_ge(ln_var, n + 1)
                v.wait_ge(dve_c, n_chain[0])
                if n >= 1:
                    v.wait_ge(xt_done, n)
                for i in range(GB):
                    ins = nc.vector.tensor_scalar(xn[:, i, :], X[:, GB * g + i, :], mv[:, i, 0:1], rstd[:, i:i + 1],
                                                  ALU.subtract, ALU.mult)
                ins.then_inc(xn_ok, 1)

            def split(f, r, p, evac, done, store, G):
                v.wait_ge(evac, 2 * (G + 1))
                if G >= 1:
                    v.wait_ge(store, 16 * G)
                link(nc.vector.tensor_tensor(r[:, :], f[:, :], p[:, 0, :], ALU.subtract))
                link(nc.vector.tensor_copy(p[:, 1, :], r[:, :]))
                nc.vector.tensor_tensor(p[:, 2, :], r[:, :], p[:, 1, :], ALU.subtract).then_inc(done, 1)

            def v_bias(G):
                L = G // NG
                v.wait_ge(v_done, G + 1)
                if G >= 1:
                    v.wait_ge(v_r, G)
                    v.wait_ge(v_1, G)
                nc.vector.tensor_tensor(vf[:, :, :], bank[7][0:SK, :].rearrange("p (b d) -> p b d", d=D),
                                        BR[0:SK, 2 * L, :].unsqueeze(1).broadcast_to([SK, GB, D]), ALU.add).then_inc(v_f, 1)

            def row_max(Bi, r):
                U = Bi * UNITS + r
                v.wait_ge(qm_done, U + 1)
                if r == 0 and Bi >= 2:
                    v.wait_ge(nm_ok, Bi - 1)
                ins = nc.vector.tensor_reduce(nmx[Bi % 2][:, UH * r:UH * r + UH],
                                              bank[U % 2][:, 0:UH * SK].rearrange("p (h k) -> p h k", k=SK),
                                              AX.X, ALU.max, negate=True)
                ins.then_inc(max_done, 1)

            def max_parts(Bi):
                i = Bi % 2
                v.wait_ge(max_done, UNITS * (Bi + 1))
                if Bi >= 1:
                    v.wait_ge(nm_ok, Bi)
                if Bi >= 2:
                    v.wait_ge(nt_done, Bi - 1)
                link(nc.vector.tensor_copy(nmp[i][:, 0, :], nmx[i][:, :]))
                link(nc.vector.tensor_tensor(nmr[:, :], nmx[i][:, :], nmp[i][:, 0, :], ALU.subtract))
                link(nc.vector.tensor_copy(nmp[i][:, 1, :], nmr[:, :]))
                nc.vector.tensor_tensor(nmp[i][:, 2, :], nmr[:, :], nmp[i][:, 1, :], ALU.subtract).then_inc(nm_ok, 1)

            def normalise(Bi):
                v.wait_ge(pv_done, Bi + 1)
                if Bi >= 1:
                    v.wait_ge(cn_ok, Bi)
                if Bi >= 2:
                    v.wait_ge(ct_done, Bi - 1)
                pv = bank[4][:, 0:H * VC].rearrange("p (h c) -> p h c", c=VC)
                link(nc.vector.tensor_reduce(num[:, :, :], pv[:, :, 0:PARTS * HD].rearrange("p h (c d) -> p h d c", d=HD), AX.X, ALU.add))
                link(nc.vector.reciprocal(rec[:, :], pv[:, :, PARTS * HD]))
                nc.vector.tensor_tensor(cn[Bi % 2][:, :].rearrange("p (h d) -> p h d", d=HD), num[:, :, :],
                                        rec[:, :].unsqueeze(2).broadcast_to([S, H, HD]), ALU.mult).then_inc(cn_ok, 1)

            def add_attention(Bi):
                b, G, k = bseq(Bi)
                v.wait_ge(op_done, Bi + 1)
                if k == 0:
                    v.wait_ge(xb_ok, G + 1)
                nc.vector.scalar_tensor_tensor(X[:, b, :], bank[6][:, 128:256], TG[:, 2 * (Bi // B):2 * (Bi // B) + 1],
                                               X[:, b, :], ALU.mult, ALU.add).then_inc(xa_ok, 1)

            v.wait_ge(w_in, 96)
            v.wait_ge(tg_ok, 1)
            for L in range(LAYERS):
                link(nc.vector.tensor_scalar(bqs[:, L:L + 1], BC[:, 2 * L:2 * L + 1], SCALE, None, ALU.mult))
                link(nc.vector.tensor_scalar(tgbo[:, L, :], BR[:, 2 * L + 1, :], TG[:, 2 * L:2 * L + 1], None, ALU.mult))
            nc.vector.tensor_scalar(mu1[:, :], BC[:, 9:11], -1.0, 1.0, ALU.mult, ALU.add).then_inc(consts_ok, 1)
            split(kf, kr, kp, k_evac, k_split, k_st, 0)
            v_bias(0)
            ln(0, 0)
            v.wait_ge(m_in, 16)
            nc.vector.tensor_scalar(MB[:, :, :], MU8[:, :, :], MASKED, None, ALU.mult).then_inc(mb_ok, 1)
            ln_apply(0, 0)
            split(qf, qr, qp, q_evac, q_split, q_st, 0)

            def moe_gate(g):
                v.wait_ge(sg_ok, g + 1)
                if g == 0:
                    v.wait_ge(w_in2, 64)
                    v.wait_ge(pool_c, 7)
                if g >= 1:
                    v.wait_ge(gt_done, g)
                bc = lambda t: t.unsqueeze(2).broadcast_to([S, GB, E])
                link(nc.vector.tensor_scalar(sc[:, :, :], sc[:, :, :], GA[:, 4:5], None, ALU.mult))
                for k, (src, m, oh) in enumerate(((sc, m1, oh1), (s2, m2, oh2))):
                    link(nc.vector.tensor_reduce(m[:, :], src[:, :, :], AX.X, ALU.max))
                    link(nc.vector.tensor_tensor(eq[:, :, :], src[:, :, :], bc(m[:, :]), ALU.is_equal))
                    link(nc.vector.tensor_tensor(eq[:, :, :], eq[:, :, :], RANK[:, :, :], ALU.mult))
                    link(nc.vector.tensor_reduce(mw[:, :], eq[:, :, :], AX.X, ALU.max))
                    link(nc.vector.tensor_tensor(oh[:, :, :], eq[:, :, :], bc(mw[:, :]), ALU.is_equal))
                    if k == 0:
                        link(nc.vector.scalar_tensor_tensor(s2[:, :, :], oh1[:, :, :], -1e30, sc[:, :, :], ALU.mult, ALU.add))
                link(nc.vector.tensor_tensor(den[:, :], m1[:, :], m2[:, :], ALU.add))
                link(nc.vector.reciprocal(den[:, :], den[:, :]))
                link(nc.vector.tensor_tensor(gw[:, :, 0], m1[:, :], den[:, :], ALU.mult))
                link(nc.vector.tensor_tensor(gw[:, :, 1], m2[:, :], den[:, :], ALU.mult))
                link(nc.vector.tensor_tensor(oh1[:, :, :], oh1[:, :, :], bc(gw[:, :, 0]), ALU.mult))
                link(nc.vector.tensor_tensor(oh2[:, :, :], oh2[:, :, :], bc(gw[:, :, 1]), ALU.mult))
                gg = gx[:, :, HID:HID + E]
                link(nc.vector.tensor_tensor(gg, oh1[:, :, :], oh2[:, :, :], ALU.add))
                link(nc.vector.tensor_copy(gp[:, :, 0, :], gg))
                link(nc.vector.tensor_tensor(gr[:, :, :], gg, gp[:, :, 0, :], ALU.subtract))
                link(nc.vector.tensor_copy(gp[:, :, 1, :], gr[:, :, :]))
                nc.vector.tensor_tensor(gp[:, :, 2, :], gr[:, :, :], gp[:, :, 1, :], ALU.subtract).then_inc(g_ok, 1)

            def gate_hidden(g, k):
                i = g * NBLK + k
                v.wait_ge(gb_done, i + 1)
                v.wait_ge(h_act, g * (NBLK + 1) + k + 1)
                if g >= 1:
                    v.wait_ge(y_done, g)
                nc.vector.tensor_tensor(hs[:, k, :], bank[2 + i % 2][:, :], hT[:, i % 2, :], ALU.mult).then_inc(hs_ok, 1)

            def add_moe(g):
                v.wait_ge(y_done, g + 1)
                xg = X[:, GB * g:GB * g + GB, :]
                nc.vector.scalar_tensor_tensor(xg, bank[4][:, :].rearrange("p (b d) -> p b d", d=D), TG[:, 1:2], xg,
                                               ALU.mult, ALU.add).then_inc(xf_ok, 1)

            for L in range(LAYERS):
                for s in range(B + 5):
                    G = L * NG + s // GB + 1
                    live = s < B and G < LAYERS * NG
                    liveq = live and G != NG
                    k = s % GB
                    if s < B:
                        row_max(L * B + s, 0)
                    if 5 <= s:
                        add_attention(L * B + s - 5)
                    if liveq and k == 0:
                        ln(2 * (G // NG), G % NG)
                    if s < B:
                        row_max(L * B + s, 1)
                    if live and k == 1:
                        split(kf, kr, kp, k_evac, k_split, k_st, G)
                    if s < B:
                        row_max(L * B + s, 2)
                    if liveq and k == 0:
                        ln_apply(2 * (G // NG), G % NG)
                    if liveq and k == 2:
                        split(qf, qr, qp, q_evac, q_split, q_st, G)
                    if live and k == 3:
                        v_bias(G)
                    if 3 <= s < B + 3:
                        normalise(L * B + s - 3)
                    if s < B:
                        row_max(L * B + s, 3)
                        max_parts(L * B + s)
                if L == 0:
                    v.wait_ge(xa_ok, B)
                    ln(1, 0)
                    ln_apply(1, 0)
                    moe_gate(0)
                    for g in range(NG):
                        if g + 1 < NG:
                            ln(1, g + 1)
                            ln_apply(1, g + 1)
                        else:
                            v.wait_ge(xf_ok, 1)
                            ln(2, 0)
                            ln_apply(2, 0)
                        for k in range(NBLK):
                            gate_hidden(g, k)
                        if g == NG - 1:
                            split(qf, qr, qp, q_evac, q_split, q_st, NG)
                        if g + 1 < NG:
                            moe_gate(g + 1)
                        add_moe(g)
                    v.wait_ge(xf_ok, NG)
                else:
                    v.wait_ge(xa_ok, NB)

                    def mix(g):
                        v.wait_ge(xs_evac, g + 1)
                        for j, (t, o, w, ok) in enumerate(((tr_, xr, r_done, xr_ok), (tk_, xk, kk_done, xk_ok))):
                            v.wait_ge(mix_t, 2 * g + j + 1)
                            if g >= 1:
                                v.wait_ge(w, g)
                            nc.vector.scalar_tensor_tensor(o[:, :, :], xsh[:, :, 1:S + 1], BC[:, 9 + j:10 + j], t[:, :, :],
                                                           ALU.mult, ALU.add).then_inc(ok, 1)

                    def add_ffn(g):
                        v.wait_ge(vv_done, g + 1)
                        v.wait_ge(r_act, g + 1)
                        xg = X[:, GB * g:GB * g + GB, :]
                        link(nc.vector.scalar_tensor_tensor(yv[:, :, :], bank[1 + 3 * (g % 2)][:, :].rearrange("p (b d) -> p b d", d=D),
                                                            TG[:, 3:4], rs[:, :, :], ALU.mult, ALU.mult))
                        nc.vector.tensor_tensor(xg, xg, yv[:, :, :], ALU.add).then_inc(xo_ok, 1)

                    for g in range(NG):
                        ln(3, g)
                        ln_apply(3, g)
                        mix(g)
                        if g >= 1:
                            add_ffn(g - 1)
                    add_ffn(NG - 1)

        @block.scalar
        def _(a):
            a.wait_ge(w_in, 96)
            nc.scalar.activation(TG[:, :], GA[:, 0:4], ACT.Tanh).then_inc(tg_ok, 1)

            def xt_copy(n):
                a.wait_ge(xt_done, n + 1)
                nc.scalar.activation(xnT[:, :], bank[7 if n // NG in (0, 2) else 6][:, :], ACT.Copy).then_inc(xt_evac, 1)

            def q_copy(G):
                a.wait_ge(q_done, G + 1)
                a.wait_ge(consts_ok, 1)
                if G >= 1:
                    a.wait_ge(q_split, G)
                    a.wait_ge(q_st, 16 * G)
                L = G // NG
                nc.scalar.activation(qf[:, :], bank[7][:, :], ACT.Identity, bias=bqs[:, L:L + 1], scale=SCALE).then_inc(q_evac, 1)
                nc.scalar.activation(qp[:, 0, :], bank[7][:, :], ACT.Identity, bias=bqs[:, L:L + 1], scale=SCALE).then_inc(q_evac, 1)

            def k_copy(G):
                a.wait_ge(k_done, G + 1)
                if G >= 1:
                    a.wait_ge(k_split, G)
                    a.wait_ge(k_st, 16 * G)
                L = G // NG
                nc.scalar.activation(kf[:, :], bank[7][:, 0:GK], ACT.Identity, bias=BC[:, 2 * L + 1:2 * L + 2]).then_inc(k_evac, 1)
                nc.scalar.activation(kp[:, 0, :], bank[7][:, 0:GK], ACT.Identity, bias=BC[:, 2 * L + 1:2 * L + 2]).then_inc(k_evac, 1)

            def v_first(G):
                a.wait_ge(v_f, G + 1)
                if G >= 2:
                    a.wait_ge(pv_done, GB * (G - 1))
                nc.scalar.activation(VS[G % 2][:, :, :, 0:HD], vf[:, :, :].rearrange("p b (h d) -> p b h d", d=HD), ACT.Copy).then_inc(v_1, 1)

            def v_second(G):
                a.wait_ge(v_r, G + 1)
                nc.scalar.activation(VS[G % 2][:, :, :, HD:2 * HD], vr[:, :, :].rearrange("p b (h d) -> p b h d", d=HD), ACT.Copy).then_inc(v_2, 1)

            def nt_copy(Bi):
                a.wait_ge(nt_done, Bi + 1)
                if Bi >= 2:
                    a.wait_ge(m_ld[Bi % 2], 48 * (Bi // 2))
                nc.scalar.activation(nmT[Bi % 2][:, :], bank[5][:, :].bitcast(BF16)[0:PARTS * H, 0:S], ACT.Copy).then_inc(nt_evac, 1)

            def exps(Bi, r):
                U = Bi * UNITS + r
                i = Bi % 2
                a.wait_ge(km_done, U + 1)
                if r == 0 and Bi >= 2:
                    a.wait_ge(p2_done, 2 * (Bi - 1))
                    a.wait_ge(pv_done, Bi - 1)
                hh = slice(UH * r, UH * r + UH)
                src = bank[2 + U % 2][0:SK, :].rearrange("p (h s) -> p h s", s=S)
                nc.scalar.activation(P32[i][:, hh, :], src, ACT.Exp, bias=LIFT)
                nc.scalar.activation(P1[i][:, hh, :], src, ACT.Exp, bias=LIFT).then_inc(exp_done, 1)

            def ct_copy(Bi):
                a.wait_ge(ct_done, Bi + 1)
                if Bi >= 2:
                    a.wait_ge(op_done, Bi - 1)
                nc.scalar.activation(cT[Bi % 2][:, :], bank[6][:, 0:128], ACT.Copy).then_inc(ct_evac, 1)

            k_copy(0)
            v_first(0)
            v_second(0)
            xt_copy(0)
            q_copy(0)

            for L in range(LAYERS):
                for s in range(B + 5):
                    G = L * NG + s // GB + 1
                    live = s < B and G < LAYERS * NG
                    liveq = live and G != NG
                    k = s % GB
                    if 4 <= s < B + 4:
                        ct_copy(L * B + s - 4)
                    if 2 <= s < B + 2:
                        exps(L * B + s - 2, 0)
                    if 1 <= s < B + 1:
                        nt_copy(L * B + s - 1)
                    if 2 <= s < B + 2:
                        exps(L * B + s - 2, 1)
                    if live and k == 0:
                        k_copy(G)
                    if liveq and k == 1:
                        xt_copy(ln_no(2 * (G // NG), G % NG))
                    if 2 <= s < B + 2:
                        exps(L * B + s - 2, 2)
                        exps(L * B + s - 2, 3)
                    if liveq and k == 1:
                        q_copy(G)
                    if live and k == 3:
                        v_first(G)
                    if after_v(s, G):
                        v_second(G - 1)
                if L == 0:
                    def sigm(g):
                        a.wait_ge(lg_done, g + 1)
                        if g >= 1:
                            a.wait_ge(g_ok, g)
                        nc.scalar.activation(sc[:, :, :], bank[5][:, 0:GB * E].rearrange("p (b e) -> p b e", e=E), ACT.Sigmoid).then_inc(sg_ok, 1)

                    def gt_copy(g):
                        a.wait_ge(gt_done, g + 1)
                        nc.scalar.activation(gpT[:, :], bank[5][:, :].bitcast(BF16)[0:PARTS * E, 512:1024], ACT.Copy)
                        if g >= 1:
                            a.wait_ge(y_done, g)
                        nc.scalar.activation(h5[HID:HID + E + 1, :], bank[6][HID:HID + E + 1, :], ACT.Copy).then_inc(gt_evac, 1)

                    def gelu(g, k):
                        j = g * (NBLK + 1) + k
                        a.wait_ge(h_done, j + 1)
                        if k < NBLK:
                            i = g * NBLK + k
                            if i >= 2:
                                a.wait_ge(hs_ok, i - 1)
                            nc.scalar.activation(hT[:, i % 2, :], bank[j % 2][:, :], ACT.Gelu, bias=BC[:, 4 + k:5 + k]).then_inc(h_act, 1)
                        else:
                            nc.scalar.activation(h5[0:HID, :], bank[j % 2][0:HID, :], ACT.Gelu, bias=BC[0:HID, 8:9]).then_inc(h_act, 1)

                    xt_copy(ln_no(1, 0))
                    sigm(0)
                    for g in range(NG):
                        gt_copy(g)
                        for k in range(NBLK + 1):
                            gelu(g, k)
                        if g + 1 < NG:
                            xt_copy(ln_no(1, g + 1))
                            sigm(g + 1)
                        else:
                            xt_copy(ln_no(2, 0))
                            q_copy(NG)
                else:
                    def sh_copy(g):
                        n = ln_no(3, g)
                        a.wait_ge(xt_done, n + 1)
                        if g >= 1:
                            a.wait_ge(xk_ok, g)
                        nc.scalar.activation(xsh[:, :, 1:S + 1], bank[6][:, :].rearrange("p (b s) -> p b s", s=S), ACT.Copy).then_inc(xs_evac, 1)
                        a.wait_ge(xs_evac, g + 1)
                        for j, t in enumerate((tr_, tk_)):
                            nc.scalar.activation(t[:, :, :], xsh[:, :, 0:S], ACT.Copy, scale=mu1[:, j:j + 1]).then_inc(mix_t, 1)

                    def r_sig(g):
                        a.wait_ge(r_done, g + 1)
                        if g >= 1:
                            a.wait_ge(xo_ok, g)
                        nc.scalar.activation(rs[:, :, :], bank[2 + 3 * (g % 2)][:, :].rearrange("p (b d) -> p b d", d=D), ACT.Sigmoid).then_inc(r_act, 1)

                    def k_act(g):
                        a.wait_ge(kk_done, g + 1)
                        nc.scalar.activation(kre[:, :], bank[3 * (g % 2)][:, :], ACT.Relu).then_inc(kr_ok, 1)
                        a.wait_ge(kr_ok, g + 1)
                        if g >= 1:
                            a.wait_ge(vv_done, g)
                        nc.scalar.activation(ksq[:, :], kre[:, :], ACT.Square).then_inc(ks_ok, 1)

                    for g in range(NG):
                        sh_copy(g)
                        k_act(g)
                        r_sig(g)

        @block.tensor
        def _(pe):
            mm = nc.tensor.matmul

            def k_proj(G):
                L, g = G // NG, G % NG
                if G >= 1:
                    pe.wait_ge(v_f, G)
                if G == NG + 1:
                    pe.wait_ge(q_evac, 2 * G)
                mm(bank[7][:, 0:GK], W(WK[L]), CT[:, g * GK:(g + 1) * GK], start=True, stop=True).then_inc(k_done, 1)

            def turn(phase, g, bk):
                n = ln_no(phase, g)
                pe.wait_ge(xn_ok, n + 1)
                for i in range(GB):
                    last = nc.tensor.transpose(bank[bk][:, i * S:(i + 1) * S], xn[:, i, :], IDF[:, :])
                last.then_inc(xt_done, 1)

            def q_proj(G):
                L, g = G // NG, G % NG
                pe.wait_ge(xt_evac, ln_no(2 * L, g) + 1)
                mm(bank[7][:, :], W(WQ[L]), xnT[:, :], start=True, stop=True).then_inc(q_done, 1)

            def v_proj(G, after_q=True):
                L, g = G // NG, G % NG
                if after_q:
                    pe.wait_ge(q_evac, 2 * (G + 1))
                for i in range(GB):
                    c = (g * GB + i) * SK
                    last = mm(bank[7][0:SK, i * D:(i + 1) * D], CT[:, c:c + SK], W(WV[L]), start=True, stop=True)
                last.then_inc(v_done, 1)

            def scores_q(Bi, r):
                b, G, k = bseq(Bi)
                U = Bi * UNITS + r
                o = bank[U % 2]
                if U >= 2:
                    pe.wait_ge(max_done, U - 1)
                if r == 0 and k == 0:
                    pe.wait_ge(q_ld[G % 2], 144 * (G // 2 + 1))
                    pe.wait_ge(k_ld[G % 2], 144 * (G // 2 + 1))
                masked = Bi < B
                if masked:
                    mm(o[:, 0:UH * SK].rearrange("p (h k) -> p h k", k=SK), IDH[:, :],
                       MB[:, b, :].unsqueeze(1).broadcast_to([S, UH, SK]), start=True, stop=False, skip_group_check=True)
                for j in range(UH):
                    h = UH * r + j
                    last = mm(o[:, j * SK:(j + 1) * SK], QS[G % 2][0:STACK, h, k * S:(k + 1) * S],
                              KS[G % 2][0:STACK, h, k * SK:(k + 1) * SK], start=not masked, stop=True, skip_group_check=True)
                last.then_inc(qm_done, 1)

            def scores_k(Bi, r):
                b, G, k = bseq(Bi)
                U = Bi * UNITS + r
                o = bank[2 + U % 2]
                if U >= 2:
                    pe.wait_ge(exp_done, U - 1)
                if r == 0:
                    pe.wait_ge(m_ld[Bi % 2], 48 * (Bi // 2 + 1))
                masked = Bi < B
                if masked:
                    mm(o[0:SK, :].rearrange("p (h s) -> p h s", s=S), MB[:, b, :],
                       IDH[:, :].unsqueeze(1).broadcast_to([S, UH, S]), start=True, stop=False, skip_group_check=True)
                for j in range(UH):
                    h = UH * r + j
                    last = mm(o[0:SK, j * S:(j + 1) * S], KS[G % 2][0:ROWS, h, k * SK:(k + 1) * SK],
                              QS[G % 2][0:ROWS, h, k * S:(k + 1) * S], start=not masked, stop=True, skip_group_check=True)
                last.then_inc(km_done, 1)

            def turn_max(Bi):
                pe.wait_ge(nm_ok, Bi + 1)
                if Bi >= 1:
                    pe.wait_ge(nt_evac, Bi)
                nc.tensor.transpose(bank[5][:, :].bitcast(BF16)[0:PARTS * H, 0:S],
                                    nmp[Bi % 2][:, :, :].rearrange("p c h -> p (c h)"), IDH[:, :]).then_inc(nt_done, 1)

            def values(Bi):
                b, G, k = bseq(Bi)
                pe.wait_ge(p2_done, 2 * (Bi + 1))
                if Bi >= 1:
                    pe.wait_ge(cn_ok, Bi)
                if k == 0:
                    pe.wait_ge(v_3, G + 1)
                for h in range(H):
                    o = bank[4][:, h * VC:(h + 1) * VC]
                    mm(o, P1[Bi % 2][:, h, :], VS[G % 2][:, k, h, :], start=(h == 0), stop=False, skip_group_check=True)
                    last = mm(o, P2[Bi % 2][:, h, :], VS[G % 2][:, k, h, :], start=False, stop=True, skip_group_check=True)
                last.then_inc(pv_done, 1)

            def turn_ctx(Bi):
                pe.wait_ge(cn_ok, Bi + 1)
                if Bi >= 1:
                    pe.wait_ge(xa_ok, Bi)
                nc.tensor.transpose(bank[6][:, 0:128], cn[Bi % 2][:, :], IDF[:, :]).then_inc(ct_done, 1)

            def out_proj(Bi):
                pe.wait_ge(ct_evac, Bi + 1)
                mm(bank[6][:, 128:256], cT[Bi % 2][:, :], W(WO[Bi // B]), start=True, stop=True).then_inc(op_done, 1)

            pe.wait_ge(w_in, 96)
            pe.wait_ge(c_in, 16)
            k_proj(0)
            pe.wait_ge(k_evac, 2)
            v_proj(0, False)
            pe.wait_ge(v_f, 1)
            turn(0, 0, 7)
            q_proj(0)
            pe.wait_ge(mb_ok, 1)
            pe.wait_ge(ones_in, 32)
            pe.wait_ge(q_evac, 2)
            pe.wait_ge(pool_c, 7)

            for L in range(LAYERS):
                for s in range(B + 5):
                    G = L * NG + s // GB + 1
                    live = s < B and G < LAYERS * NG
                    liveq = live and G != NG
                    k = s % GB
                    for r in range(UNITS):
                        if s < B:
                            scores_q(L * B + s, r)
                        if 2 <= s < B + 2:
                            scores_k(L * B + s - 2, r)
                        if r == 0:
                            if 4 <= s < B + 4:
                                turn_ctx(L * B + s - 4)
                            if 1 <= s < B + 1:
                                turn_max(L * B + s - 1)
                        if r == 1:
                            if live and k == 0:
                                if G == 1:
                                    pe.wait_ge(w_in2, 64)
                                k_proj(G)
                            if liveq and k == 1:
                                pe.wait_ge(k_evac, 2 * (G + 1))
                                turn(2 * (G // NG), G % NG, 7)
                            if 3 <= s < B + 3:
                                values(L * B + s - 3)
                        if r == 2:
                            if liveq and k == 1:
                                q_proj(G)
                            if live and k == 2:
                                if G == NG:
                                    pe.wait_ge(k_evac, 2 * (G + 1))
                                v_proj(G, G != NG)
                        if r == 3:
                            if 4 <= s < B + 4:
                                out_proj(L * B + s - 4)
                if L == 0:
                    def turn_and_gate(g):
                        turn(1, g, 6)
                        pe.wait_ge(xt_evac, ln_no(1, g) + 1)
                        if g >= 1:
                            pe.wait_ge(gt_evac, g)
                        for i in range(GB):
                            last = mm(bank[5][:, i * E:(i + 1) * E], xnT[:, i * S:(i + 1) * S], W(WGATE, E), start=True, stop=True)
                        last.then_inc(lg_done, 1)

                    def turn_gates(g):
                        pe.wait_ge(g_ok, g + 1)
                        for i in range(GB):
                            nc.tensor.transpose(bank[5][:, :].bitcast(BF16)[0:PARTS * E, 512 + i * S:512 + (i + 1) * S],
                                                gp[:, i, :, :].rearrange("p c e -> p (c e)"), IDH[:, :])
                        for i in range(GB):
                            last = nc.tensor.transpose(bank[6][0:HID + E + 1, i * S:(i + 1) * S], gx[:, i, :], IDF[:, :])
                        last.then_inc(gt_done, 1)

                    pe.wait_ge(xa_ok, B)
                    turn_and_gate(0)
                    for g in range(NG):
                        turn_gates(g)
                        for k in range(NBLK + 1):
                            j = g * (NBLK + 1) + k
                            if j >= 2:
                                pe.wait_ge(h_act, j - 1)
                            if k < NBLK:
                                mm(bank[j % 2][:, :], W(W1 + k), xnT[:, :], start=True, stop=True).then_inc(h_done, 1)
                                i = g * NBLK + k
                                if k == 0:
                                    pe.wait_ge(gt_evac, g + 1)
                                if i >= 2:
                                    pe.wait_ge(hs_ok, i - 1)
                                mm(bank[2 + i % 2][:, :], SEL[:, k * 128:(k + 1) * 128], gpT[:, :], start=True, stop=True).then_inc(gb_done, 1)
                            else:
                                mm(bank[j % 2][0:HID, :], W(WSH, HID), xnT[:, :], start=True, stop=True).then_inc(h_done, 1)
                        if g + 1 < NG:
                            turn_and_gate(g + 1)
                        else:
                            pe.wait_ge(v_f, NG + 1)
                            turn(2, 0, 7)
                            q_proj(NG)
                        pe.wait_ge(hs_ok, (g + 1) * NBLK)
                        pe.wait_ge(h_act, (g + 1) * (NBLK + 1))
                        if g >= 1:
                            pe.wait_ge(xf_ok, g)
                        for i in range(GB):
                            for k in range(NBLK + 1):
                                lhs = hs[:, k, i * S:(i + 1) * S] if k < NBLK else h5[:, i * S:(i + 1) * S]
                                rhs = W(W2 + k) if k < NBLK else W2S[:, :]
                                last = mm(bank[4][:, i * D:(i + 1) * D], lhs, rhs, start=(k == 0), stop=(k == NBLK))
                        last.then_inc(y_done, 1)
                    pe.wait_ge(xf_ok, NG)
                else:
                    pe.wait_ge(xa_ok, NB)
                    for g in range(NG):
                        turn(3, g, 6)
                        pe.wait_ge(xk_ok, g + 1)
                        if g >= 2:
                            pe.wait_ge(kr_ok, g - 1)
                            pe.wait_ge(r_act, g - 1)
                            pe.wait_ge(xo_ok, g - 1)
                        mm(bank[3 * (g % 2)][:, :], W(WKK), xk[:, :, :].rearrange("p b s -> p (b s)"), start=True, stop=True).then_inc(kk_done, 1)
                        pe.wait_ge(xr_ok, g + 1)
                        for i in range(GB):
                            last = mm(bank[2 + 3 * (g % 2)][:, i * D:(i + 1) * D], xr[:, i, :], W(WR), start=True, stop=True)
                        last.then_inc(r_done, 1)
                        pe.wait_ge(ks_ok, g + 1)
                        for i in range(GB):
                            last = mm(bank[1 + 3 * (g % 2)][:, i * D:(i + 1) * D], ksq[:, i * S:(i + 1) * S], W(WVV), start=True, stop=True)
                        last.then_inc(vv_done, 1)


def kernel(**inputs):
    import numpy as np
    import ml_dtypes
    import concourse.bacc as bacc
    from concourse import mybir as mb
    from concourse.bass_utils import run_bass_kernel_spmd as run

    a = {k: np.asarray(v) for k, v in inputs.items()}
    f = np.float32

    def pad(w):
        o = np.zeros((128, 128), f)
        o[:w.shape[0], :w.shape[1]] = w
        return o

    w1 = a["L0_ffn_W1"].transpose(1, 0, 2).reshape(D, E * HID)
    w2 = a["L0_ffn_W2"].reshape(E * HID, D)
    blocks = [a["L0_xattn_Wq"], a["L0_xattn_Wk"], a["L0_xattn_Wv"], a["L0_xattn_Wo"],
              a["L1_xattn_Wq"].T, a["L1_xattn_Wk"].T, a["L1_xattn_Wv"].T, a["L1_xattn_Wo"].T]
    blocks += [w1[:, 128 * i:128 * i + 128] for i in range(NBLK)]
    blocks += [pad(a["L0_ffn_Ws1"]), pad(a["L0_ffn_gate_W"])]
    blocks += [w2[128 * i:128 * i + 128, :] for i in range(NBLK)]
    blocks += [a["L1_ffn_W_r"].T, a["L1_ffn_W_k"].T, a["L1_ffn_W_v"].T]
    b1 = a["L0_ffn_b1"].reshape(NBLK, 128)
    bs1 = np.zeros(128, f)
    bs1[:HID] = a["L0_ffn_bs1"]
    cols = [a["L0_xattn_bq"], a["L0_xattn_bk"], a["L1_xattn_bq"], a["L1_xattn_bk"], *b1, bs1,
            a["L1_ffn_mu_r"], a["L1_ffn_mu_k"]]
    sel = np.zeros((PARTS, E, NBLK, 2, HID), ml_dtypes.bfloat16)
    for e in range(E):
        sel[:, e, e // 2, e % 2, :] = 1
    arrays = {
        "x": a["x"],
        "ctxT": a["ctx_1024"].reshape(B * SK, D).T,
        "mask": a["mask_Bx1xSxS2_bk1"].reshape(B, S, SK),
        "wts": np.concatenate(blocks, axis=1),
        "w2sh": np.concatenate([a["L0_ffn_Ws2"], a["L0_ffn_b2"], a["L0_ffn_bs2"][None]], axis=0),
        "bcols": np.stack(cols, axis=1),
        "brows": np.stack([a["L0_xattn_bv"], a["L0_xattn_bo"], a["L1_xattn_bv"], a["L1_xattn_bo"]])[None],
        "gates": np.stack([a["g_xattn"][0], a["g_ffn"][0], a["g_xattn"][1], a["g_ffn"][1],
                           a["L0_ffn_route_scale"].reshape(())])[None],
        "ident": np.eye(128, dtype=f),
        "identh": np.eye(128, dtype=f).astype(ml_dtypes.bfloat16),
        "sel": sel.reshape(PARTS * E, NBLK * 128),
        "rank": np.broadcast_to(np.arange(E, 0, -1, dtype=f), (128, GB, E)),
        "onesrows": np.ones((PARTS, H, GK), ml_dtypes.bfloat16),
    }
    nc = bacc.Bacc("TRN2", target_bir_lowering=False, num_devices=1)
    named, args = {}, []
    for name, v in arrays.items():
        v = np.ascontiguousarray(v)
        named[f"in_{name}"] = v
        args.append(nc.dram_tensor(f"in_{name}", v.shape, mb.dt.from_np(v.dtype), kind="ExternalInput").ap())
    out = nc.dram_tensor("out_0", (B, S, D), mb.dt.float32, kind="ExternalOutput").ap()
    gated_blocks(nc, *args, out)
    r = run(nc, [named], core_ids=[0])
    return r.results[0]["out_0"]
```

```python
import concourse.bass as bass
from concourse import mybir
from contextlib import ExitStack

F32 = mybir.dt.float32
BF16 = mybir.dt.bfloat16
FP16 = mybir.dt.float16
U8 = mybir.dt.uint8
ALU = mybir.AluOpType
ACT = mybir.ActivationFunctionType
AX = mybir.AxisListType

B, S, SK, D = 16, 128, 120, 128
H, HD = 16, 8
E, HID = 8, 64
PARTS = 3
STACK = PARTS * PARTS * HD
ROWS = STACK + PARTS
VC = PARTS * HD + 1
NG, GB = 4, 4
GT, GK = GB * S, GB * SK
UNITS, UH = 4, 4
LAYERS = 2
MASKED = -float(2 ** 50)
EPS = 1e-5
SCALE = float(HD) ** -0.5
K_STEPS, Q_STEPS, V_STEPS, TURN_STEP = (1, 3, 6), (5, 7, 9), (8, 11, 13), 4
LAG = 10
LIFT = 6.931471805599453
NBLK = E * HID // 128


def gated_blocks(nc, x, ctxT, mask, wts, w2sh, bcols, brows, gates, ident, identh, negidh, sel, rank, onesrows, out):
    ctx = ExitStack()
    with ctx:
        def sb(name, shape, dt=F32):
            return ctx.enter_context(nc.sbuf_tensor(name, shape, dt))

        def sem(name):
            return ctx.enter_context(nc.semaphore(name))

        X = sb("X", [S, B, D])
        CT = sb("CT", [D, B * SK])
        WT = sb("WT", [128, 21 * 128])
        W2S = sb("W2S", [HID + E + 1, 128])
        BC = sb("BC", [128, 13])
        BR = sb("BR", [128, LAYERS, 128])
        GA = sb("GA", [128, 5])
        TG = sb("TG", [128, 4])
        IDF = sb("IDF", [128, 128])
        IDH = sb("IDH", [128, 128], BF16)
        NEG = sb("NEG", [128, 128], BF16)
        SEL = sb("SEL", [PARTS * E, NBLK * 128], BF16)
        RANK = sb("RANK", [128, B, E])
        MU8 = sb("MU8", [S, B, SK], U8)
        MB = sb("MB", [S, B, SK], BF16)
        tgbo = sb("tgbo", [128, LAYERS, 128])
        mu1 = sb("mu1", [128, 2])
        epsT = sb("epsT", [128, GB])
        powT = sb("powT", [128, GB])
        st6 = sb("st6", [S, GB, 6])
        mv = sb("mv", [S, GB, 2])
        ve = sb("ve", [S, GB])
        rstd = sb("rstd", [S, GB])
        xn = sb("xn", [S, GB, D])
        xnT = sb("xnT", [D, GT])
        qp = sb("qp", [128, PARTS, GT], BF16)
        kp = sb("kp", [128, PARTS, GK], BF16)
        QS = [sb(f"QS{i}", [ROWS, 2, H, GT // 2], BF16) for i in range(2)]
        KS = [sb(f"KS{i}", [ROWS, 2, H, GK // 2], BF16) for i in range(2)]
        VS = [sb(f"VS{i}", [SK, GB, H, VC], BF16) for i in range(3)]
        nmx = [sb(f"nmx{i}", [S, H]) for i in range(2)]
        nmr = sb("nmr", [S, H])
        nmp = [sb(f"nmp{i}", [S, PARTS, H], BF16) for i in range(2)]
        nmT = [sb(f"nmT{i}", [PARTS * H, S], BF16) for i in range(2)]
        P32 = [sb(f"P32{i}", [SK, H, S]) for i in range(2)]
        P1 = [sb(f"P1{i}", [SK, H, S], FP16) for i in range(2)]
        P2 = [sb(f"P2{i}", [SK, H, S], FP16) for i in range(2)]
        num = sb("num", [S, H, HD])
        rec = sb("rec", [S, H])
        cn = [sb(f"cn{i}", [S, D]) for i in range(2)]
        cT = [sb(f"cT{i}", [D, S]) for i in range(2)]
        XT4 = sb("XT4", [D, NG, GT])
        FF = sb("FF", [128, 10, GT])
        hT = FF[:, 0:NBLK, :]
        hs = FF[:, NBLK:2 * NBLK, :]
        h5 = [FF[0:HID + E + 1, 2 * NBLK + i, :] for i in range(2)]
        sc = sb("sc", [S, B, E])
        m1 = sb("m1", [S, B])
        m2 = sb("m2", [S, B])
        eq = sb("eq", [S, B, E])
        mw = sb("mw", [S, B])
        oh1 = sb("oh1", [S, B, E])
        oh2 = sb("oh2", [S, B, E])
        s2 = sb("s2", [S, B, E])
        den = sb("den", [S, B])
        gw = sb("gw", [S, B, 2])
        gr = sb("gr", [S, B, E])
        gp = sb("gp", [S, B, PARTS, E], BF16)
        gx = sb("gx", [S, B, HID + E + 1])
        gpT = sb("gpT", [PARTS * E, GT], BF16)
        xsh = sb("xsh", [D, B, S + 1])
        tr_ = FF[:, 0, :].rearrange("p (b s) -> p b s", s=S)
        tk_ = FF[:, 1, :].rearrange("p (b s) -> p b s", s=S)
        xr = FF[:, 2, :].rearrange("p (b s) -> p b s", s=S)
        xk = FF[:, 3, :].rearrange("p (b s) -> p b s", s=S)
        rs = FF[:, 4, :].rearrange("p (b d) -> p b d", d=D)
        kre = FF[:, 5, :]
        ksq = FF[:, 6, :]
        yv = [FF[:, 7 + i, :].rearrange("p (b d) -> p b d", d=D) for i in range(2)]

        bank = [ctx.enter_context(nc.psum_tensor(f"bank{i}", [128, 512], F32)) for i in range(8)]
        qparts = nc.dram_tensor("qparts", [2, 2, PARTS, HD, H, GT // 2], BF16).ap()
        kparts = nc.dram_tensor("kparts", [2, 2, PARTS, HD, H, GK // 2], BF16).ap()

        def W(i, n=128):
            return WT[:, i * 128:i * 128 + n]

        WQ, WK, WV, WO = [0, 4], [1, 5], [2, 6], [3, 7]
        W1, WSH, WGATE, W2, WR, WKK, WVV = 8, 12, 13, 14, 18, 19, 20

        x_in = [sem(f"x_in{i}") for i in range(NG)]
        w_in = sem("w_in"); w_in2 = sem("w_in2"); c_in = sem("c_in"); m_in = sem("m_in")
        ones_in = sem("ones_in")
        tg_ok = sem("tg_ok"); consts_ok = sem("consts_ok"); mb_ok = sem("mb_ok")
        pool_c = sem("pool_c")
        dve_c = sem("dve_c")
        act_c = sem("act_c")
        ln_var = sem("ln_var"); ln_rstd = sem("ln_rstd"); xn_ok = sem("xn_ok"); xb_ok = sem("xb_ok")
        xt_done = sem("xt_done"); xt_evac = sem("xt_evac")
        q_done = sem("q_done"); q_evac = sem("q_evac")
        q_st = sem("q_st"); q_ld = [[sem(f"q_ld{i}{f}") for f in range(2)] for i in range(2)]
        k_done = sem("k_done"); k_evac = sem("k_evac")
        k_st = sem("k_st"); k_ld = [[sem(f"k_ld{i}{f}") for f in range(2)] for i in range(2)]
        v_done = sem("v_done"); v_evac = sem("v_evac"); bo_done = sem("bo_done"); bo_ok = sem("bo_ok")
        qm_done = sem("qm_done"); max_done = sem("max_done"); nm_ok = sem("nm_ok")
        nt_done = sem("nt_done"); nt_evac = sem("nt_evac"); m_ld = [sem("m_ld0"), sem("m_ld1")]
        km_done = sem("km_done"); exp_done = sem("exp_done"); p2_done = sem("p2_done")
        pv_done = sem("pv_done"); cn_ok = sem("cn_ok"); ct_done = sem("ct_done"); ct_evac = sem("ct_evac")
        op_done = sem("op_done"); xa_ok = sem("xa_ok")
        lg_done = sem("lg_done"); sg_ok = sem("sg_ok"); g_ok = sem("g_ok"); gt_done = sem("gt_done"); gt_evac = sem("gt_evac")
        h_done = sem("h_done"); h_act = sem("h_act"); gb_done = sem("gb_done"); hs_ok = sem("hs_ok")
        y_done = sem("y_done"); xf_ok = sem("xf_ok")
        xs_evac = sem("xs_evac"); mix_t = sem("mix_t"); xr_ok = sem("xr_ok"); xk_ok = sem("xk_ok")
        r_done = sem("r_done"); r_act = sem("r_act"); kk_done = sem("kk_done"); kr_ok = sem("kr_ok"); ks_ok = sem("ks_ok")
        vv_done = sem("vv_done"); y_ok = sem("y_ok"); xo_ok = sem("xo_ok"); o_out = sem("o_out")

        block = ctx.enter_context(nc.Block())

        def bseq(Bi):
            return Bi % B, Bi // GB, Bi % GB

        NB = LAYERS * B
        KVB = bank[6]
        QB = bank[7]

        def prep_at(L, s):
            g, p = divmod(s + 5, GB)
            G = L * NG + g
            return (G, p) if g <= NG and G < LAYERS * NG else (None, None)

        def ffn_norm_at(s):
            g, r = divmod(s - 10, GB)
            return g if s >= 10 and r == 0 and g < NG - 1 else None

        LN_ORDER = [(0, 0), (0, 1), (0, 2), (0, 3), (1, 0), (1, 1), (1, 2), (1, 3),
                    (2, 0), (2, 1), (2, 2), (2, 3), (3, 0), (3, 1), (3, 2), (3, 3)]

        def ln_no(phase, g):
            return LN_ORDER.index((phase, g))

        @block.sync
        def _(sp):
            for g in range(NG):
                sp.dma_start(X[:, GB * g:GB * g + GB, :], x[GB * g:GB * g + GB, :, :].rearrange("b s d -> s b d")).then_inc(x_in[g], 16)
                if g == 0:
                    sp.dma_start(CT[:, :], ctxT).then_inc(c_in, 16)
                    sp.dma_start(WT[:, 0:4 * 128], wts[:, 0:4 * 128]).then_inc(w_in, 16)
                    sp.dma_start(BC[:, :], bcols).then_inc(w_in, 16)
                    sp.dma_start(IDF[:, :], ident).then_inc(w_in, 16)
                    sp.dma_start(GA[:, :], gates.broadcast_to([128, 5])).then_inc(w_in, 16)
                    sp.dma_start(NEG[:, :], negidh).then_inc(w_in, 16)
                    sp.dma_start(BR[:, :, :], brows.broadcast_to([128, LAYERS, 128])).then_inc(w_in, 16)
                    sp.dma_start(IDH[:, :], identh).then_inc(w_in, 16)
                    sp.dma_start(MU8[:, :, :], mask.rearrange("b s k -> s b k")).then_inc(m_in, 16)
                    for i in range(2):
                        sp.dma_start(KS[i][STACK:ROWS, :, :, :], onesrows).then_inc(ones_in, 16)
            sp.dma_start(WT[:, 4 * 128:], wts[:, 4 * 128:]).then_inc(w_in2, 16)
            sp.dma_start(W2S[:, :], w2sh).then_inc(w_in2, 16)
            sp.dma_start(SEL[:, :], sel).then_inc(w_in2, 16)
            sp.dma_start(RANK[:, :, :], rank).then_inc(w_in2, 16)

            def k_store(G):
                sp.wait_ge(k_evac, PARTS * (G + 1))
                if G >= 2:
                    for f in range(2):
                        sp.wait_ge(k_ld[G % 2][f], 16 * PARTS * (G // 2))
                for p in range(PARTS):
                    sp.dma_start(kparts[G % 2, :, p].rearrange("f d h t -> (d h) f t"), kp[:, p, :].rearrange("r (f t) -> r f t", f=2)).then_inc(k_st, 16)

            def k_load(G, f):
                sp.wait_ge(k_st, 16 * PARTS * (G + 1))
                if G >= 2:
                    sp.wait_ge(km_done, (GB * (G - 2) + 2 * (f + 1)) * UNITS)
                src = kparts[G % 2, f].rearrange("c d h t -> (c d) h t")
                n = PARTS * HD
                for a in range(PARTS):
                    sp.dma_start(KS[G % 2][a * n:(a + 1) * n, f, :, :], src).then_inc(k_ld[G % 2][f], 16)

            def q_store(G):
                sp.wait_ge(q_evac, PARTS * (G + 1))
                if G >= 2:
                    for f in range(2):
                        sp.wait_ge(q_ld[G % 2][f], 16 * PARTS * (G // 2))
                for p in range(PARTS):
                    sp.dma_start(qparts[G % 2, :, p].rearrange("f d h t -> (d h) f t"), qp[:, p, :].rearrange("r (f t) -> r f t", f=2)).then_inc(q_st, 16)

            def q_load(G, f):
                sp.wait_ge(q_st, 16 * PARTS * (G + 1))
                if G >= 2:
                    sp.wait_ge(km_done, (GB * (G - 2) + 2 * (f + 1)) * UNITS)
                n = PARTS * HD
                for a in range(PARTS):
                    sp.dma_start(QS[G % 2][a * n:(a + 1) * n, f, :, :],
                                 qparts[G % 2, f, a].unsqueeze(0).broadcast_to([PARTS, HD, H, GT // 2])).then_inc(q_ld[G % 2][f], 16)

            def max_rows(Bi):
                b, G, k = bseq(Bi)
                sp.wait_ge(nt_evac, Bi + 1)
                if G >= 2 and k % 2 == 0:
                    sp.wait_ge(km_done, (GB * (G - 2) + k + 2) * UNITS)
                for p in range(PARTS):
                    sp.dma_start(QS[G % 2][STACK + p:STACK + p + 1, k // 2, :, (k % 2) * S:(k % 2 + 1) * S],
                                 nmT[Bi % 2][p * H:(p + 1) * H, :]).then_inc(m_ld[Bi % 2], 16)

            k_store(0)
            k_load(0, 0)
            q_store(0)
            q_load(0, 0)
            k_load(0, 1)
            q_load(0, 1)
            for L in range(LAYERS):
                for s in range(B + 1):
                    if s >= 1:
                        max_rows(L * B + s - 1)
                    G, p = prep_at(L, s)
                    if G is not None and p == 1:
                        k_store(G)
                    if G is not None and p == 2:
                        k_load(G, 0)
                        if G != NG:
                            q_store(G)
                            q_load(G, 0)
                    if G is not None and p == 3:
                        k_load(G, 1)
                        if G != NG:
                            q_load(G, 1)
                if L == 0:
                    q_store(NG)
                    q_load(NG, 0)
                    q_load(NG, 1)
            for g in range(NG):
                sp.wait_ge(xo_ok, g + 1)
                sp.dma_start(out[GB * g:GB * g + GB, :, :].rearrange("b s d -> s b d"), X[:, GB * g:GB * g + GB, :]).then_inc(o_out, 16)
            sp.wait_ge(o_out, 16 * NG)

        @block.gpsimd
        def _(po):
            po.memset(epsT[:, :], EPS).then_inc(pool_c, 1)
            po.memset(powT[:, :], -0.5).then_inc(pool_c, 1)
            for i in range(3):
                po.memset(VS[i][:, :, :, PARTS * HD:VC], 1.0).then_inc(pool_c, 1)
            po.memset(gx[:, :, :], 0.0).then_inc(pool_c, 1)
            po.memset(xsh[:, :, 0:1], 0.0).then_inc(pool_c, 1)
            po.wait_ge(pool_c, 7)
            po.memset(gx[:, :, HID + E:], 1.0).then_inc(pool_c, 1)

            def ln_rstd_(n):
                po.wait_ge(ln_var, n + 1)
                po.tensor_tensor(ve[:, :], mv[:, :, 1], epsT[:, :], ALU.add).then_inc(ln_rstd, 1)
                po.wait_ge(ln_rstd, 2 * n + 1)
                po.tensor_tensor(rstd[:, :], ve[:, :], powT[:, :], ALU.pow).then_inc(ln_rstd, 1)

            def bias_on_x(G):
                L, g = G // NG, G % NG
                po.wait_ge(xn_ok, ln_no(2 * L, g) + 1)
                po.wait_ge(bo_ok, L + 1)
                xg = X[:, GB * g:GB * g + GB, :]
                po.tensor_tensor(xg, xg, tgbo[:, L, :].unsqueeze(1).broadcast_to([S, GB, D]), ALU.add).then_inc(xb_ok, 1)

            def p_low(Bi, half):
                po.wait_ge(exp_done, Bi * UNITS + 2 * half + 2)
                if Bi >= 2:
                    po.wait_ge(pv_done, Bi - 1)
                hh = slice(8 * half, 8 * half + 8)
                po.tensor_tensor(P2[Bi % 2][:, hh, :], P32[Bi % 2][:, hh, :], P1[Bi % 2][:, hh, :], ALU.subtract).then_inc(p2_done, 1)

            def add_ffn_low(g):
                po.wait_ge(y_ok, g + 1)
                xg = X[:, GB * g:GB * g + GB, :]
                po.tensor_tensor(xg, xg, yv[g % 2][:, :, :], ALU.add).then_inc(xo_ok, 1)

            ln_rstd_(ln_no(0, 0))
            for L in range(LAYERS):
                ln_rstd_(ln_no(2 * L, 1))
                for s in range(B + 6):
                    G, p = prep_at(L, s)
                    if p == 0 and G != NG:
                        ln_rstd_(ln_no(2 * L, G % NG))
                    if ffn_norm_at(s) is not None:
                        ln_rstd_(ln_no(2 * L + 1, ffn_norm_at(s)))
                    if 3 <= s < B + 3:
                        p_low(L * B + s - 3, 0)
                    if s < B and s % GB == 1:
                        bias_on_x(L * NG + s // GB)
                    if 3 <= s < B + 3:
                        p_low(L * B + s - 3, 1)
                ln_rstd_(ln_no(2 * L + 1, NG - 1))
                if L == 0:
                    ln_rstd_(ln_no(2, 0))
                else:
                    for g in range(NG):
                        add_ffn_low(g)

        @block.vector
        def _(v):
            n_chain = [0]

            def mark(ins):
                n_chain[0] += 1
                ins.then_inc(dve_c, 1)
                return n_chain[0]

            def link(ins):
                v.wait_ge(dve_c, mark(ins))

            def ln(phase, g):
                n = ln_no(phase, g)
                if phase == 0:
                    v.wait_ge(x_in[g], 16)
                if phase in (1, 3):
                    v.wait_ge(xa_ok, B * (phase // 2) + GB * (g + 1))
                if phase == 2:
                    v.wait_ge(xf_ok, g + 1)
                if n >= 1:
                    v.wait_ge(ln_rstd, 2 * n)
                for i in range(GB):
                    nc.vector.bn_stats(st6[:, i, :], X[:, GB * g + i, :]).then_inc(dve_c, 1)
                n_chain[0] += GB
                v.wait_ge(dve_c, n_chain[0])
                for i in range(GB):
                    ins = nc.vector.bn_aggr(mv[:, i, :], st6[:, i, :])
                    if i < GB - 1:
                        ins.then_inc(dve_c, 1)
                n_chain[0] += GB - 1
                ins.then_inc(ln_var, 1)

            def ln_apply(phase, g):
                n = ln_no(phase, g)
                v.wait_ge(ln_rstd, 2 * n + 2)
                v.wait_ge(ln_var, n + 1)
                v.wait_ge(dve_c, n_chain[0])
                if n >= 1:
                    v.wait_ge(xt_done, n)
                for i in range(GB):
                    ins = nc.vector.tensor_scalar(xn[:, i, :], X[:, GB * g + i, :], mv[:, i, 0:1], rstd[:, i:i + 1],
                                                  ALU.subtract, ALU.mult)
                ins.then_inc(xn_ok, 1)

            def row_max(Bi, r):
                U = Bi * UNITS + r
                v.wait_ge(qm_done, U + 1)
                if r == 0 and Bi >= 2:
                    v.wait_ge(nm_ok, Bi - 1)
                ins = nc.vector.tensor_reduce(nmx[Bi % 2][:, UH * r:UH * r + UH],
                                              bank[U % 2][:, 0:UH * SK].rearrange("p (h k) -> p h k", k=SK),
                                              AX.X, ALU.max, negate=True)
                ins.then_inc(max_done, 1)

            def parts_and_normalise(Bi, Bn):
                a = Bi is not None
                c = Bn is not None
                if a:
                    i = Bi % 2
                    v.wait_ge(max_done, UNITS * (Bi + 1))
                    if Bi >= 1:
                        v.wait_ge(nm_ok, Bi)
                    if Bi >= 2:
                        v.wait_ge(nt_done, Bi - 1)
                    first = mark(nc.vector.tensor_copy(nmp[i][:, 0, :], nmx[i][:, :]))
                if c:
                    v.wait_ge(pv_done, Bn + 1)
                    if Bn >= 1:
                        v.wait_ge(cn_ok, Bn)
                    if Bn >= 2:
                        v.wait_ge(ct_done, Bn - 1)
                    pv = bank[4][:, 0:H * VC].rearrange("p (h c) -> p h c", c=VC)
                    mark(nc.vector.tensor_reduce(num[:, :, :], pv[:, :, 0:PARTS * HD].rearrange("p h (c d) -> p h d c", d=HD), AX.X, ALU.add))
                if a:
                    v.wait_ge(dve_c, first)
                    second = mark(nc.vector.tensor_tensor(nmr[:, :], nmx[i][:, :], nmp[i][:, 0, :], ALU.subtract))
                if c:
                    total = mark(nc.vector.reciprocal(rec[:, :], pv[:, :, PARTS * HD]))
                if a:
                    v.wait_ge(dve_c, second)
                    third = mark(nc.vector.tensor_copy(nmp[i][:, 1, :], nmr[:, :]))
                if c:
                    v.wait_ge(dve_c, total)
                    nc.vector.tensor_tensor(cn[Bn % 2][:, :].rearrange("p (h d) -> p h d", d=HD), num[:, :, :],
                                            rec[:, :].unsqueeze(2).broadcast_to([S, H, HD]), ALU.mult).then_inc(cn_ok, 1)
                if a:
                    v.wait_ge(dve_c, third)
                    nc.vector.tensor_tensor(nmp[i][:, 2, :], nmr[:, :], nmp[i][:, 1, :], ALU.subtract).then_inc(nm_ok, 1)

            def add_attention(Bi):
                b, G, k = bseq(Bi)
                v.wait_ge(op_done, Bi + 1)
                if k == 0:
                    v.wait_ge(xb_ok, G + 1)
                nc.vector.scalar_tensor_tensor(X[:, b, :], bank[5][:, 0:128], TG[:, 2 * (Bi // B):2 * (Bi // B) + 1],
                                               X[:, b, :], ALU.mult, ALU.add).then_inc(xa_ok, 1)

            def bias_row(L):
                v.wait_ge(bo_done, LAYERS)
                link(nc.vector.tensor_tensor(tgbo[:, L, :], bank[4][:, 128 * L:128 * L + 128], BR[:, L, :], ALU.add))
                nc.vector.tensor_scalar(tgbo[:, L, :], tgbo[:, L, :], TG[:, 2 * L:2 * L + 1], None, ALU.mult).then_inc(bo_ok, 1)

            def last_k(G):
                v.wait_ge(k_done, PARTS * (G + 1))
                L = G // NG
                nc.vector.tensor_scalar(kp[:, PARTS - 1, :], KVB[:, 0:GK], BC[:, 2 * L + 1:2 * L + 2], None, ALU.add).then_inc(k_evac, 1)

            def last_q(G):
                v.wait_ge(q_done, PARTS * (G + 1))
                L = G // NG
                nc.vector.tensor_scalar(qp[:, PARTS - 1, :], QB[:, :], BC[:, 2 * L:2 * L + 1], None, ALU.add).then_inc(q_evac, 1)

            def last_v(G):
                v.wait_ge(v_done, PARTS * (G + 1))
                nc.vector.tensor_copy(VS[G % 3][:, :, :, 2 * HD:3 * HD],
                                      KVB[0:SK, :].rearrange("p (b h d) -> p b h d", h=H, d=HD)).then_inc(v_evac, 1)

            v.wait_ge(w_in, 112)
            v.wait_ge(tg_ok, 1)
            nc.vector.tensor_scalar(mu1[:, :], BC[:, 9:11], -1.0, 1.0, ALU.mult, ALU.add).then_inc(consts_ok, 1)
            ln(0, 0)
            v.wait_ge(m_in, 16)
            nc.vector.tensor_scalar(MB[:, :, :], MU8[:, :, :], MASKED, None, ALU.mult).then_inc(mb_ok, 1)
            ln_apply(0, 0)
            last_k(0)
            last_v(0)
            last_q(0)

            def moe_gate():
                v.wait_ge(sg_ok, 1)
                v.wait_ge(w_in2, 64)
                v.wait_ge(pool_c, 8)
                bc = lambda t: t.unsqueeze(2).broadcast_to([S, B, E])
                link(nc.vector.tensor_scalar(sc[:, :, :], sc[:, :, :], GA[:, 4:5], None, ALU.mult))
                for k, (src, m, oh) in enumerate(((sc, m1, oh1), (s2, m2, oh2))):
                    link(nc.vector.tensor_reduce(m[:, :], src[:, :, :], AX.X, ALU.max))
                    link(nc.vector.tensor_tensor(eq[:, :, :], src[:, :, :], bc(m[:, :]), ALU.is_equal))
                    link(nc.vector.tensor_tensor(eq[:, :, :], eq[:, :, :], RANK[:, :, :], ALU.mult))
                    link(nc.vector.tensor_reduce(mw[:, :], eq[:, :, :], AX.X, ALU.max))
                    link(nc.vector.tensor_tensor(oh[:, :, :], eq[:, :, :], bc(mw[:, :]), ALU.is_equal))
                    if k == 0:
                        link(nc.vector.scalar_tensor_tensor(s2[:, :, :], oh1[:, :, :], -1e30, sc[:, :, :], ALU.mult, ALU.add))
                link(nc.vector.tensor_tensor(den[:, :], m1[:, :], m2[:, :], ALU.add))
                link(nc.vector.reciprocal(den[:, :], den[:, :]))
                link(nc.vector.tensor_tensor(gw[:, :, 0], m1[:, :], den[:, :], ALU.mult))
                link(nc.vector.tensor_tensor(gw[:, :, 1], m2[:, :], den[:, :], ALU.mult))
                link(nc.vector.tensor_tensor(oh1[:, :, :], oh1[:, :, :], bc(gw[:, :, 0]), ALU.mult))
                link(nc.vector.tensor_tensor(oh2[:, :, :], oh2[:, :, :], bc(gw[:, :, 1]), ALU.mult))
                gg = gx[:, :, HID:HID + E]
                link(nc.vector.tensor_tensor(gg, oh1[:, :, :], oh2[:, :, :], ALU.add))
                link(nc.vector.tensor_copy(gp[:, :, 0, :], gg))
                link(nc.vector.tensor_tensor(gr[:, :, :], gg, gp[:, :, 0, :], ALU.subtract))
                link(nc.vector.tensor_copy(gp[:, :, 1, :], gr[:, :, :]))
                nc.vector.tensor_tensor(gp[:, :, 2, :], gr[:, :, :], gp[:, :, 1, :], ALU.subtract).then_inc(g_ok, 1)

            def gate_hidden(g, k):
                i = g * NBLK + k
                v.wait_ge(gb_done, i + 1)
                v.wait_ge(h_act, g * (NBLK + 1) + k + 1)
                if g >= 1:
                    v.wait_ge(y_done, g)
                nc.vector.tensor_tensor(hs[:, k, :], bank[2 + i % 2][:, :], hT[:, k, :], ALU.mult).then_inc(hs_ok, 1)

            def add_moe(g):
                v.wait_ge(y_done, g + 1)
                xg = X[:, GB * g:GB * g + GB, :]
                nc.vector.scalar_tensor_tensor(xg, bank[4][:, :].rearrange("p (b d) -> p b d", d=D), TG[:, 1:2], xg,
                                               ALU.mult, ALU.add).then_inc(xf_ok, 1)

            for L in range(LAYERS):
                ln(2 * L, 1)
                ln_apply(2 * L, 1)
                if L == 0:
                    bias_row(0)
                    bias_row(1)
                for s in range(B + 6):
                    G, p = prep_at(L, s)
                    norm = None
                    if p == 0 and G != NG:
                        norm = (2 * L, G % NG)
                    if ffn_norm_at(s) is not None:
                        norm = (2 * L + 1, ffn_norm_at(s))
                    for r in range(UNITS):
                        u = UNITS * p + r if G is not None else None
                        if u == K_STEPS[2] + 1:
                            last_k(G)
                        if u == Q_STEPS[2] + 1 and G != NG:
                            last_q(G)
                        if u == V_STEPS[2] + 1:
                            last_v(G)
                        if s < B:
                            row_max(L * B + s, r)
                        if norm and r == 0:
                            ln(*norm)
                        if r == 1 and s >= 6:
                            add_attention(L * B + s - 6)
                        if norm and r == 2:
                            ln_apply(*norm)
                    parts_and_normalise(L * B + s if s < B else None, L * B + s - 4 if 4 <= s < B + 4 else None)
                ln(2 * L + 1, NG - 1)
                ln_apply(2 * L + 1, NG - 1)
                if L == 0:
                    moe_gate()
                    for g in range(NG):
                        for k in range(NBLK):
                            gate_hidden(g, k)
                        if g >= 1:
                            add_moe(g - 1)
                            if g == 1:
                                ln(2, 0)
                                ln_apply(2, 0)
                            if g == 2:
                                last_q(NG)
                    add_moe(NG - 1)
                else:
                    def mix(g):
                        for j, (t, o, w, ok) in enumerate(((tr_, xr, r_done, xr_ok), (tk_, xk, kk_done, xk_ok))):
                            v.wait_ge(mix_t, 2 * g + j + 1)
                            if g >= 1:
                                v.wait_ge(w, g)
                            nc.vector.scalar_tensor_tensor(o[:, :, :], xsh[:, GB * g:GB * g + GB, 1:S + 1], BC[:, 9 + j:10 + j], t[:, :, :],
                                                           ALU.mult, ALU.add).then_inc(ok, 1)

                    def add_ffn(g):
                        v.wait_ge(vv_done, g + 1)
                        v.wait_ge(r_act, g + 1)
                        if g >= 2:
                            v.wait_ge(xo_ok, g - 1)
                        nc.vector.scalar_tensor_tensor(yv[g % 2][:, :, :], bank[1 + 3 * (g % 2)][:, :].rearrange("p (b d) -> p b d", d=D),
                                                            TG[:, 3:4], rs[:, :, :], ALU.mult, ALU.mult).then_inc(y_ok, 1)

                    mix(0)
                    for g in range(NG):
                        if g + 1 < NG:
                            mix(g + 1)
                        if g >= 1:
                            add_ffn(g - 1)
                    add_ffn(NG - 1)

        @block.scalar
        def _(a):
            a.wait_ge(w_in, 112)
            nc.scalar.activation(TG[:, :], GA[:, 0:4], ACT.Tanh).then_inc(tg_ok, 1)

            def xt_copy(phase, g):
                n = ln_no(phase, g)
                a.wait_ge(xt_done, n + 1)
                src = (KVB if phase in (1, 3) else QB)[:, :]
                if phase == 1:
                    nc.scalar.activation(XT4[:, g, :], src, ACT.Copy).then_inc(xt_evac, 1)
                elif phase == 3:
                    nc.scalar.activation(xsh[:, GB * g:GB * g + GB, 1:S + 1], src.rearrange("p (b s) -> p b s", s=S), ACT.Copy).then_inc(xt_evac, 1)
                else:
                    nc.scalar.activation(xnT[:, :], src, ACT.Copy).then_inc(xt_evac, 1)

            def q_part(G, p):
                a.wait_ge(q_done, PARTS * G + p + 1)
                if G >= 1 and p == 0:
                    a.wait_ge(q_st, 16 * PARTS * G)
                L = G // NG
                nc.scalar.activation(qp[:, p, :], QB[:, :], ACT.Identity, bias=BC[:, 2 * L:2 * L + 1]).then_inc(q_evac, 1)

            def k_part(G, p):
                a.wait_ge(k_done, PARTS * G + p + 1)
                if G >= 1 and p == 0:
                    a.wait_ge(k_st, 16 * PARTS * G)
                L = G // NG
                nc.scalar.activation(kp[:, p, :], KVB[:, 0:GK], ACT.Identity, bias=BC[:, 2 * L + 1:2 * L + 2]).then_inc(k_evac, 1)

            def v_part(G, p):
                a.wait_ge(v_done, PARTS * G + p + 1)
                if G >= 3 and p == 0:
                    a.wait_ge(pv_done, GB * (G - 2))
                nc.scalar.activation(VS[G % 3][:, :, :, p * HD:(p + 1) * HD],
                                     KVB[0:SK, :].rearrange("p (b h d) -> p b h d", h=H, d=HD), ACT.Copy).then_inc(v_evac, 1)

            def nt_copy(Bi):
                a.wait_ge(nt_done, Bi + 1)
                if Bi >= 2:
                    a.wait_ge(m_ld[Bi % 2], 48 * (Bi // 2))
                nc.scalar.activation(nmT[Bi % 2][:, :], bank[5][:, :].bitcast(BF16)[0:PARTS * H, 0:S], ACT.Copy).then_inc(nt_evac, 1)

            def exps(Bi, r):
                U = Bi * UNITS + r
                i = Bi % 2
                a.wait_ge(km_done, U + 1)
                if r == 0 and Bi >= 2:
                    a.wait_ge(p2_done, 2 * (Bi - 1))
                    a.wait_ge(pv_done, Bi - 1)
                hh = slice(UH * r, UH * r + UH)
                src = bank[2 + U % 2][0:SK, :].rearrange("p (h s) -> p h s", s=S)
                nc.scalar.activation(P32[i][:, hh, :], src, ACT.Exp, bias=LIFT, scale=SCALE)
                nc.scalar.activation(P1[i][:, hh, :], src, ACT.Exp, bias=LIFT, scale=SCALE).then_inc(exp_done, 1)

            def ct_copy(Bi):
                a.wait_ge(ct_done, Bi + 1)
                if Bi >= 2:
                    a.wait_ge(op_done, Bi - 1)
                nc.scalar.activation(cT[Bi % 2][:, :], bank[5][:, 0:128], ACT.Copy).then_inc(ct_evac, 1)

            def prep(G, u):
                for p in range(PARTS - 1):
                    if u == K_STEPS[p] + 1:
                        k_part(G, p)
                    if u == Q_STEPS[p] + 1 and G != NG:
                        q_part(G, p)
                    if u == V_STEPS[p] + 1:
                        v_part(G, p)
                if u == TURN_STEP + 1 and G != NG:
                    xt_copy(2 * (G // NG), G % NG)

            for p in range(PARTS - 1):
                k_part(0, p)
            for p in range(PARTS - 1):
                v_part(0, p)
            xt_copy(0, 0)
            for p in range(PARTS - 1):
                q_part(0, p)

            for L in range(LAYERS):
                for u in range(UNITS):
                    prep(L * NG + 1, u)
                for s in range(B + 6):
                    G, p = prep_at(L, s)
                    for r in range(UNITS):
                        if G is not None:
                            prep(G, UNITS * p + r)
                        if r == 2 and 1 <= s < B + 1:
                            nt_copy(L * B + s - 1)
                        if r == 0 and 6 <= s:
                            ct_copy(L * B + s - 6)
                        U = UNITS * s + r - LAG
                        if 0 <= U < B * UNITS:
                            exps(L * B + U // UNITS, U % UNITS)
                        if r == 3 and ffn_norm_at(s) is not None:
                            xt_copy(2 * L + 1, ffn_norm_at(s))
                xt_copy(2 * L + 1, NG - 1)
                if L == 0:
                    a.wait_ge(lg_done, 1)
                    nc.scalar.activation(sc[:, :, :], bank[5][:, 0:B * E].rearrange("p (b e) -> p b e", e=E), ACT.Sigmoid).then_inc(sg_ok, 1)

                    def gt_copy(g):
                        a.wait_ge(gt_done, g + 1)
                        nc.scalar.activation(gpT[:, :], bank[5][:, :].bitcast(BF16)[0:PARTS * E, 512:1024], ACT.Copy)
                        if g >= 2:
                            a.wait_ge(y_done, g - 1)
                        nc.scalar.activation(h5[g % 2][HID:HID + E + 1, :], bank[6][HID:HID + E + 1, :], ACT.Copy).then_inc(gt_evac, 1)

                    def gelu(g, k):
                        j = g * (NBLK + 1) + k
                        a.wait_ge(h_done, j + 1)
                        if k < NBLK:
                            i = g * NBLK + k
                            if i >= NBLK:
                                a.wait_ge(hs_ok, i - NBLK + 1)
                            nc.scalar.activation(hT[:, k, :], bank[j % 2][:, :], ACT.Gelu, bias=BC[:, 4 + k:5 + k]).then_inc(h_act, 1)
                        else:
                            if g >= 2:
                                a.wait_ge(y_done, g - 1)
                            nc.scalar.activation(h5[g % 2][0:HID, :], bank[j % 2][0:HID, :], ACT.Gelu, bias=BC[0:HID, 8:9]).then_inc(h_act, 1)

                    for k in range(NBLK + 1):
                        gelu(0, k)
                    for g in range(NG):
                        gt_copy(g)
                        if g + 1 < NG:
                            for k in range(NBLK + 1):
                                gelu(g + 1, k)
                        if g == 2:
                            xt_copy(2, 0)
                            for p in range(PARTS - 1):
                                q_part(NG, p)
                else:
                    def sh_copy(g):
                        n = ln_no(3, g)
                        a.wait_ge(xt_evac, n + 1)
                        for j, (t, ok) in enumerate(((tr_, xr_ok), (tk_, xk_ok))):
                            if g >= 1:
                                a.wait_ge(ok, g)
                            nc.scalar.activation(t[:, :, :], xsh[:, GB * g:GB * g + GB, 0:S], ACT.Copy, scale=mu1[:, j:j + 1]).then_inc(mix_t, 1)

                    def r_sig(g):
                        a.wait_ge(r_done, g + 1)
                        if g >= 1:
                            a.wait_ge(y_ok, g)
                        nc.scalar.activation(rs[:, :, :], bank[2 + 3 * (g % 2)][:, :].rearrange("p (b d) -> p b d", d=D), ACT.Sigmoid).then_inc(r_act, 1)

                    def k_act(g):
                        a.wait_ge(kk_done, g + 1)
                        nc.scalar.activation(kre[:, :], bank[3 * (g % 2)][:, :], ACT.Relu).then_inc(kr_ok, 1)
                        a.wait_ge(kr_ok, g + 1)
                        if g >= 1:
                            a.wait_ge(vv_done, g)
                        nc.scalar.activation(ksq[:, :], kre[:, :], ACT.Square).then_inc(ks_ok, 1)

                    sh_copy(0)
                    for g in range(NG):
                        if g + 1 < NG:
                            sh_copy(g + 1)
                        k_act(g)
                        r_sig(g)

        @block.tensor
        def _(pe):
            mm = nc.tensor.matmul

            kv_reader = [None]
            q_reader = [None]

            def bank_read(reader):
                if reader[0]:
                    pe.wait_ge(*reader[0])

            def k_proj(G, p):
                L, g = G // NG, G % NG
                if p == 0:
                    bank_read(kv_reader)
                    mm(KVB[:, 0:GK], W(WK[L]), CT[:, g * GK:(g + 1) * GK], start=True, stop=True).then_inc(k_done, 1)
                    kv_reader[0] = (k_evac, PARTS * (G + 1))
                else:
                    pe.wait_ge(k_evac, PARTS * G + p)
                    mm(KVB[:, 0:GK], NEG[:, :], kp[:, p - 1, :], start=False, stop=True, skip_group_check=True).then_inc(k_done, 1)

            def turn(phase, g):
                n = ln_no(phase, g)
                o, reader = (KVB, kv_reader) if phase in (1, 3) else (QB, q_reader)
                bank_read(reader)
                pe.wait_ge(xn_ok, n + 1)
                for i in range(GB):
                    last = nc.tensor.transpose(o[:, i * S:(i + 1) * S], xn[:, i, :], IDF[:, :])
                last.then_inc(xt_done, 1)
                reader[0] = (xt_evac, n + 1)

            def q_proj(G, p):
                L, g = G // NG, G % NG
                if p == 0:
                    bank_read(q_reader)
                    mm(QB[:, :], W(WQ[L]), xnT[:, :], start=True, stop=True).then_inc(q_done, 1)
                    q_reader[0] = (q_evac, PARTS * (G + 1))
                else:
                    pe.wait_ge(q_evac, PARTS * G + p)
                    mm(QB[:, :], NEG[:, :], qp[:, p - 1, :], start=False, stop=True, skip_group_check=True).then_inc(q_done, 1)

            def v_proj(G, p):
                L, g = G // NG, G % NG
                if p == 0:
                    bank_read(kv_reader)
                    for i in range(GB):
                        c = (g * GB + i) * SK
                        last = mm(KVB[0:SK, i * D:(i + 1) * D], CT[:, c:c + SK], W(WV[L]), start=(i == 0), stop=True, skip_group_check=True)
                    last.then_inc(v_done, 1)
                    kv_reader[0] = (v_evac, PARTS * (G + 1))
                else:
                    pe.wait_ge(v_evac, PARTS * G + p)
                    mm(KVB[0:SK, :].rearrange("p (b h d) -> p b h d", h=H, d=HD), NEG[0:SK, 0:SK],
                       VS[G % 3][:, :, :, (p - 1) * HD:p * HD], start=False, stop=True, skip_group_check=True).then_inc(v_done, 1)

            def bias_product(L):
                mm(bank[4][:, 128 * L:128 * L + 128], BC[:, 11 + L:12 + L].broadcast_to([128, 128]), W(WO[L]), start=True, stop=True).then_inc(bo_done, 1)

            def scores_q(Bi, r):
                b, G, k = bseq(Bi)
                U = Bi * UNITS + r
                o = bank[U % 2]
                if U >= 2:
                    pe.wait_ge(max_done, U - 1)
                if r == 0 and k % 2 == 0:
                    pe.wait_ge(q_ld[G % 2][k // 2], 16 * PARTS * (G // 2 + 1))
                    pe.wait_ge(k_ld[G % 2][k // 2], 16 * PARTS * (G // 2 + 1))
                masked = Bi < B
                if masked:
                    mm(o[:, 0:UH * SK].rearrange("p (h k) -> p h k", k=SK), IDH[:, :],
                       MB[:, b, :].unsqueeze(1).broadcast_to([S, UH, SK]), start=True, stop=False, skip_group_check=True)
                for j in range(UH):
                    h = UH * r + j
                    last = mm(o[:, j * SK:(j + 1) * SK], QS[G % 2][0:STACK, k // 2, h, (k % 2) * S:(k % 2 + 1) * S],
                              KS[G % 2][0:STACK, k // 2, h, (k % 2) * SK:(k % 2 + 1) * SK], start=not masked, stop=True, skip_group_check=True)
                last.then_inc(qm_done, 1)

            def scores_k(Bi, r):
                b, G, k = bseq(Bi)
                U = Bi * UNITS + r
                o = bank[2 + U % 2]
                if U >= 2:
                    pe.wait_ge(exp_done, U - 1)
                if r == 0:
                    pe.wait_ge(m_ld[Bi % 2], 48 * (Bi // 2 + 1))
                masked = Bi < B
                if masked:
                    mm(o[0:SK, :].rearrange("p (h s) -> p h s", s=S), MB[:, b, :],
                       IDH[:, :].unsqueeze(1).broadcast_to([S, UH, S]), start=True, stop=False, skip_group_check=True)
                for j in range(UH):
                    h = UH * r + j
                    last = mm(o[0:SK, j * S:(j + 1) * S], KS[G % 2][0:ROWS, k // 2, h, (k % 2) * SK:(k % 2 + 1) * SK],
                              QS[G % 2][0:ROWS, k // 2, h, (k % 2) * S:(k % 2 + 1) * S], start=not masked, stop=True, skip_group_check=True)
                last.then_inc(km_done, 1)

            def turn_max(Bi):
                pe.wait_ge(nm_ok, Bi + 1)
                if Bi >= 1:
                    pe.wait_ge(nt_evac, Bi)
                if Bi % B >= 5:
                    pe.wait_ge(xa_ok, Bi - 4)
                elif Bi >= B:
                    pe.wait_ge(xa_ok, B)
                nc.tensor.transpose(bank[5][:, :].bitcast(BF16)[0:PARTS * H, 0:S],
                                    nmp[Bi % 2][:, :, :].rearrange("p c h -> p (c h)"), IDH[:, :]).then_inc(nt_done, 1)

            def values(Bi, half):
                b, G, k = bseq(Bi)
                if half == 1:
                    for h in range(H // 2, H):
                        last = value_head(Bi, h)
                    last.then_inc(pv_done, 1)
                    return
                pe.wait_ge(p2_done, 2 * (Bi + 1))
                if Bi >= 1:
                    pe.wait_ge(cn_ok, Bi)
                if Bi == 0:
                    pe.wait_ge(bo_ok, LAYERS)
                if k == 0:
                    pe.wait_ge(v_evac, PARTS * (G + 1))
                for h in range(H // 2):
                    value_head(Bi, h)

            def value_head(Bi, h):
                b, G, k = bseq(Bi)
                o = bank[4][:, h * VC:(h + 1) * VC]
                mm(o, P1[Bi % 2][:, h, :], VS[G % 3][:, k, h, :], start=(h == 0), stop=False, skip_group_check=True)
                return mm(o, P2[Bi % 2][:, h, :], VS[G % 3][:, k, h, :], start=False, stop=True, skip_group_check=True)

            def turn_ctx(Bi):
                pe.wait_ge(cn_ok, Bi + 1)
                pe.wait_ge(nt_evac, min(Bi + 5, B * (Bi // B + 1)))
                if Bi % B >= 1:
                    pe.wait_ge(xa_ok, Bi)
                nc.tensor.transpose(bank[5][:, 0:128], cn[Bi % 2][:, :], IDF[:, :]).then_inc(ct_done, 1)

            def out_proj(Bi):
                pe.wait_ge(ct_evac, Bi + 1)
                mm(bank[5][:, 0:128], cT[Bi % 2][:, :], W(WO[Bi // B]), start=True, stop=True).then_inc(op_done, 1)

            def prep(G, u):
                if u in K_STEPS:
                    k_proj(G, K_STEPS.index(u))
                if u == TURN_STEP and G != NG:
                    turn(2 * (G // NG), G % NG)
                if u in Q_STEPS and G != NG:
                    q_proj(G, Q_STEPS.index(u))
                if u in V_STEPS:
                    v_proj(G, V_STEPS.index(u))

            pe.wait_ge(w_in, 112)
            pe.wait_ge(c_in, 16)
            for p in range(PARTS):
                k_proj(0, p)
            pe.wait_ge(pool_c, 8)
            for p in range(PARTS):
                v_proj(0, p)
            turn(0, 0)
            for p in range(PARTS):
                q_proj(0, p)
            pe.wait_ge(w_in2, 64)
            bias_product(0)
            bias_product(1)
            pe.wait_ge(mb_ok, 1)
            pe.wait_ge(ones_in, 32)

            for L in range(LAYERS):
                for u in range(UNITS):
                    prep(L * NG + 1, u)
                for s in range(B + 6):
                    G, p = prep_at(L, s)
                    for r in range(UNITS):
                        if s < B:
                            scores_q(L * B + s, r)
                        if r == 2 and 1 <= s < B + 1:
                            turn_max(L * B + s - 1)
                        U = UNITS * s + r - LAG
                        if 0 <= U < B * UNITS:
                            scores_k(L * B + U // UNITS, U % UNITS)
                        if r == 1 and 6 <= s:
                            out_proj(L * B + s - 6)
                        if r <= 1 and 4 <= s < B + 4:
                            values(L * B + s - 4, r)
                        if r == 3 and 5 <= s < B + 5:
                            turn_ctx(L * B + s - 5)
                        if G is not None:
                            prep(G, UNITS * p + r)
                        if r == 3 and ffn_norm_at(s) is not None:
                            turn(2 * L + 1, ffn_norm_at(s))
                turn(2 * L + 1, NG - 1)
                if L == 0:
                    pe.wait_ge(xt_evac, ln_no(1, NG - 1) + 1)
                    for b in range(B):
                        last = mm(bank[5][:, b * E:(b + 1) * E], XT4[:, b // GB, (b % GB) * S:(b % GB + 1) * S], W(WGATE, E), start=True, stop=True)
                    last.then_inc(lg_done, 1)

                    def hidden(g, k):
                        j = g * (NBLK + 1) + k
                        if j >= 2:
                            pe.wait_ge(h_act, j - 1)
                        if k < NBLK:
                            mm(bank[j % 2][:, :], W(W1 + k), XT4[:, g, :], start=True, stop=True).then_inc(h_done, 1)
                        else:
                            mm(bank[j % 2][0:HID, :], W(WSH, HID), XT4[:, g, :], start=True, stop=True).then_inc(h_done, 1)

                    def turn_gates(g):
                        pe.wait_ge(g_ok, 1)
                        if g >= 1:
                            pe.wait_ge(gt_evac, g)
                        for i in range(GB):
                            nc.tensor.transpose(bank[5][:, :].bitcast(BF16)[0:PARTS * E, 512 + i * S:512 + (i + 1) * S],
                                                gp[:, GB * g + i, :, :].rearrange("p c e -> p (c e)"), IDH[:, :])
                        for i in range(GB):
                            last = nc.tensor.transpose(bank[6][0:HID + E + 1, i * S:(i + 1) * S], gx[:, GB * g + i, :], IDF[:, :])
                        last.then_inc(gt_done, 1)

                    pe.wait_ge(xa_ok, B)
                    for k in range(NBLK + 1):
                        hidden(0, k)
                    for g in range(NG):
                        turn_gates(g)
                        for k in range(NBLK + 1):
                            i = g * NBLK + k
                            if k < NBLK:
                                if k == 0:
                                    pe.wait_ge(gt_evac, g + 1)
                                if i >= 2:
                                    pe.wait_ge(hs_ok, i - 1)
                                mm(bank[2 + i % 2][:, :], SEL[:, k * 128:(k + 1) * 128], gpT[:, :], start=True, stop=True).then_inc(gb_done, 1)
                            if g + 1 < NG:
                                hidden(g + 1, k)
                        if g == 2:
                            turn(2, 0)
                            for p in range(PARTS):
                                q_proj(NG, p)
                        pe.wait_ge(hs_ok, (g + 1) * NBLK)
                        pe.wait_ge(h_act, (g + 1) * (NBLK + 1))
                        if g >= 1:
                            pe.wait_ge(xf_ok, g)
                        for i in range(GB):
                            for k in range(NBLK + 1):
                                lhs = hs[:, k, i * S:(i + 1) * S] if k < NBLK else h5[g % 2][:, i * S:(i + 1) * S]
                                rhs = W(W2 + k) if k < NBLK else W2S[:, :]
                                last = mm(bank[4][:, i * D:(i + 1) * D], lhs, rhs, start=(k == 0), stop=(k == NBLK))
                        last.then_inc(y_done, 1)
                    pe.wait_ge(xf_ok, NG)
                    kv_reader[0] = (gt_evac, NG)
                else:
                    pe.wait_ge(xa_ok, NB)
                    for g in range(NG):
                        pe.wait_ge(xk_ok, g + 1)
                        if g >= 2:
                            pe.wait_ge(kr_ok, g - 1)
                            pe.wait_ge(r_act, g - 1)
                            pe.wait_ge(y_ok, g - 1)
                        mm(bank[3 * (g % 2)][:, :], W(WKK), xk[:, :, :].rearrange("p b s -> p (b s)"), start=True, stop=True).then_inc(kk_done, 1)
                        pe.wait_ge(xr_ok, g + 1)
                        for i in range(GB):
                            last = mm(bank[2 + 3 * (g % 2)][:, i * D:(i + 1) * D], xr[:, i, :], W(WR), start=True, stop=True)
                        last.then_inc(r_done, 1)
                        pe.wait_ge(ks_ok, g + 1)
                        for i in range(GB):
                            last = mm(bank[1 + 3 * (g % 2)][:, i * D:(i + 1) * D], ksq[:, i * S:(i + 1) * S], W(WVV), start=True, stop=True)
                        last.then_inc(vv_done, 1)


def kernel(**inputs):
    import numpy as np
    import ml_dtypes
    import concourse.bacc as bacc
    from concourse import mybir as mb
    from concourse.bass_utils import run_bass_kernel_spmd as run

    a = {k: np.asarray(v) for k, v in inputs.items()}
    f = np.float32

    def pad(w):
        o = np.zeros((128, 128), f)
        o[:w.shape[0], :w.shape[1]] = w
        return o

    w1 = a["L0_ffn_W1"].transpose(1, 0, 2).reshape(D, E * HID)
    w2 = a["L0_ffn_W2"].reshape(E * HID, D)
    def by_feature(w):
        return w.reshape(*w.shape[:-1], H, HD).swapaxes(-1, -2).reshape(w.shape)

    blocks = [by_feature(a["L0_xattn_Wq"]), by_feature(a["L0_xattn_Wk"]), a["L0_xattn_Wv"], a["L0_xattn_Wo"],
              by_feature(a["L1_xattn_Wq"].T), by_feature(a["L1_xattn_Wk"].T), a["L1_xattn_Wv"].T, a["L1_xattn_Wo"].T]
    blocks += [w1[:, 128 * i:128 * i + 128] for i in range(NBLK)]
    blocks += [pad(a["L0_ffn_Ws1"]), pad(a["L0_ffn_gate_W"])]
    blocks += [w2[128 * i:128 * i + 128, :] for i in range(NBLK)]
    blocks += [a["L1_ffn_W_r"].T, a["L1_ffn_W_k"].T, a["L1_ffn_W_v"].T]
    b1 = a["L0_ffn_b1"].reshape(NBLK, 128)
    bs1 = np.zeros(128, f)
    bs1[:HID] = a["L0_ffn_bs1"]
    cols = [*(by_feature(a[f"L{i}_xattn_b{x}"]) for i in range(LAYERS) for x in "qk"), *b1, bs1,
            a["L1_ffn_mu_r"], a["L1_ffn_mu_k"], a["L0_xattn_bv"], a["L1_xattn_bv"]]
    sel = np.zeros((PARTS, E, NBLK, 2, HID), ml_dtypes.bfloat16)
    for e in range(E):
        sel[:, e, e // 2, e % 2, :] = 1
    arrays = {
        "x": a["x"],
        "ctxT": a["ctx_1024"].reshape(B * SK, D).T,
        "mask": a["mask_Bx1xSxS2_bk1"].reshape(B, S, SK),
        "wts": np.concatenate(blocks, axis=1),
        "w2sh": np.concatenate([a["L0_ffn_Ws2"], a["L0_ffn_b2"], a["L0_ffn_bs2"][None]], axis=0),
        "bcols": np.stack(cols, axis=1),
        "brows": np.stack([a["L0_xattn_bo"], a["L1_xattn_bo"]])[None],
        "gates": np.stack([a["g_xattn"][0], a["g_ffn"][0], a["g_xattn"][1], a["g_ffn"][1],
                           a["L0_ffn_route_scale"].reshape(())])[None],
        "ident": np.eye(128, dtype=f),
        "identh": np.eye(128, dtype=f).astype(ml_dtypes.bfloat16),
        "negidh": -np.eye(128, dtype=f).astype(ml_dtypes.bfloat16),
        "sel": sel.reshape(PARTS * E, NBLK * 128),
        "rank": np.broadcast_to(np.arange(E, 0, -1, dtype=f), (128, B, E)),
        "onesrows": np.ones((PARTS, 2, H, GK // 2), ml_dtypes.bfloat16),
    }
    nc = bacc.Bacc("TRN2", target_bir_lowering=False, num_devices=1)
    named, args = {}, []
    for name, v in arrays.items():
        v = np.ascontiguousarray(v)
        named[f"in_{name}"] = v
        args.append(nc.dram_tensor(f"in_{name}", v.shape, mb.dt.from_np(v.dtype), kind="ExternalInput").ap())
    out = nc.dram_tensor("out_0", (B, S, D), mb.dt.float32, kind="ExternalOutput").ap()
    gated_blocks(nc, *args, out)
    r = run(nc, [named], core_ids=[0])
    return r.results[0]["out_0"]
```

```python
import concourse.bass as bass
from concourse import mybir
from contextlib import ExitStack

F32 = mybir.dt.float32
BF16 = mybir.dt.bfloat16
FP16 = mybir.dt.float16
U8 = mybir.dt.uint8
ALU = mybir.AluOpType
ACT = mybir.ActivationFunctionType
AX = mybir.AxisListType

B, S, SK, D = 16, 128, 120, 128
H, HD = 16, 8
E, HID = 8, 64
PARTS = 3
STACK = PARTS * PARTS * HD
ROWS = STACK + PARTS
VC = PARTS * HD + 1
NG, GB = 4, 4
GT, GK = GB * S, GB * SK
UNITS, UH = 4, 4
LAYERS = 2
MASKED = -float(2 ** 50)
EPS = 1e-5
SCALE = float(HD) ** -0.5
K_STEPS, Q_STEPS, V_STEPS, TURN_STEP = (1, 4, 5), (5, 6, 8), (10, 11, 12), 3
VALUE_STEPS = (0, 1)
LAG = 10
LIFT = 6.931471805599453
NBLK = E * HID // 128


def gated_blocks(nc, x, ctxT, mask, wts, w2sh, bcols, brows, gates, ident, identh, negidh, sel, rank, onesrows, out):
    ctx = ExitStack()
    with ctx:
        def sb(name, shape, dt=F32):
            return ctx.enter_context(nc.sbuf_tensor(name, shape, dt))

        def sem(name):
            return ctx.enter_context(nc.semaphore(name))

        X = sb("X", [S, B, D])
        CT = sb("CT", [D, B * SK])
        WT = sb("WT", [128, 21 * 128])
        W2S = sb("W2S", [HID + E + 1, 128])
        BC = sb("BC", [128, 13])
        BR = sb("BR", [128, LAYERS, 128])
        GA = sb("GA", [128, 5])
        TG = sb("TG", [128, 4])
        IDF = sb("IDF", [128, 128])
        IDH = sb("IDH", [128, 128], BF16)
        NEG = sb("NEG", [128, 128], BF16)
        SEL = sb("SEL", [PARTS * E, NBLK * 128], BF16)
        RANK = sb("RANK", [128, B, E])
        MU8 = sb("MU8", [S, B, SK], U8)
        MB = sb("MB", [S, B, SK], BF16)
        tgbo = sb("tgbo", [128, LAYERS, 128])
        epsT = sb("epsT", [128, GB])
        powT = sb("powT", [128, GB])
        st6 = sb("st6", [S, GB, 6])
        mv = sb("mv", [S, GB, 2])
        ve = sb("ve", [S, GB])
        rstd = sb("rstd", [S, GB])
        xn = sb("xn", [S, GB, D])
        xnT = sb("xnT", [D, GT])
        qp = sb("qp", [128, PARTS, GT], BF16)
        kp = sb("kp", [128, PARTS, GK], BF16)
        QS = [sb(f"QS{i}", [ROWS, 2, H, GT // 2], BF16) for i in range(2)]
        KS = [sb(f"KS{i}", [ROWS, 2, H, GK // 2], BF16) for i in range(2)]
        VS = [sb(f"VS{i}", [SK, GB, H, VC], BF16) for i in range(3)]
        nmx = [sb(f"nmx{i}", [S, H]) for i in range(2)]
        nmr = sb("nmr", [S, H])
        nmp = [sb(f"nmp{i}", [S, PARTS, H], BF16) for i in range(2)]
        nmT = [sb(f"nmT{i}", [PARTS * H, S], BF16) for i in range(2)]
        P32 = [sb(f"P32{i}", [SK, H, S]) for i in range(2)]
        P1 = [sb(f"P1{i}", [SK, H, S], FP16) for i in range(3)]
        P2 = [sb(f"P2{i}", [SK, H, S], FP16) for i in range(3)]
        num = sb("num", [S, H, HD])
        rec = sb("rec", [S, H])
        cn = [sb(f"cn{i}", [S, D]) for i in range(2)]
        cT = [sb(f"cT{i}", [D, S]) for i in range(2)]
        XT4 = sb("XT4", [D, NG, GT])
        FF = sb("FF", [128, 10, GT])
        hT = FF[:, 0:NBLK, :]
        hs = FF[:, NBLK:2 * NBLK, :]
        h5 = [FF[0:HID + E + 1, 2 * NBLK + i, :] for i in range(2)]
        sc = sb("sc", [S, B, E])
        m1 = sb("m1", [S, B])
        m2 = sb("m2", [S, B])
        eq = sb("eq", [S, B, E])
        mw = sb("mw", [S, B])
        oh1 = sb("oh1", [S, B, E])
        oh2 = sb("oh2", [S, B, E])
        s2 = sb("s2", [S, B, E])
        den = sb("den", [S, B])
        gr = sb("gr", [S, B, E])
        gp = sb("gp", [S, B, PARTS, E], BF16)
        gx = sb("gx", [S, B, HID + E + 1])
        gpT = sb("gpT", [PARTS * E, GT], BF16)
        xsh = sb("xsh", [D, B, S + 1])
        feature = lambda i: FF[:, i, :].rearrange("p (b s) -> p b s", s=S)
        xd = feature(0)
        xr = [feature(1), feature(2)]
        xk = [feature(3), feature(4)]
        rs = feature(5)
        kre = FF[:, 6, :]
        ksq = FF[:, 7, :]
        yv = [feature(8), feature(9)]

        bank = [ctx.enter_context(nc.psum_tensor(f"bank{i}", [128, 512], F32)) for i in range(8)]
        qparts = nc.dram_tensor("qparts", [2, 2, PARTS, HD, H, GT // 2], BF16).ap()
        kparts = nc.dram_tensor("kparts", [2, 2, PARTS, HD, H, GK // 2], BF16).ap()

        def W(i, n=128):
            return WT[:, i * 128:i * 128 + n]

        WQ, WK, WV, WO = [0, 4], [1, 5], [2, 6], [3, 7]
        W1, WSH, WGATE, W2, WR, WKK, WVV = 8, 12, 13, 14, 18, 19, 20

        x_in = [sem(f"x_in{i}") for i in range(NG)]
        w_in = sem("w_in"); w_in1 = sem("w_in1"); c_in2 = sem("c_in2"); w_in2 = sem("w_in2"); c_in = sem("c_in"); m_in = sem("m_in")
        ones_in = sem("ones_in")
        tg_ok = sem("tg_ok"); mb_ok = sem("mb_ok")
        pool_c = sem("pool_c")
        dve_c = sem("dve_c")
        ln_var = sem("ln_var"); ln_rstd = sem("ln_rstd"); xn_ok = sem("xn_ok"); xb_ok = sem("xb_ok")
        xt_done = sem("xt_done"); xt_evac = sem("xt_evac")
        q_done = sem("q_done"); q_evac = sem("q_evac")
        q_st = sem("q_st"); q_ld = [[sem(f"q_ld{i}{f}") for f in range(2)] for i in range(2)]
        k_done = sem("k_done"); k_evac = sem("k_evac")
        k_st = sem("k_st"); k_ld = [[sem(f"k_ld{i}{f}") for f in range(2)] for i in range(2)]
        v_done = sem("v_done"); v_evac = sem("v_evac"); bo_done = sem("bo_done"); bo_ok = sem("bo_ok")
        qm_done = sem("qm_done"); max_done = sem("max_done"); nm_ok = sem("nm_ok")
        nt_done = sem("nt_done"); nt_evac = sem("nt_evac"); m_ld = [sem("m_ld0"), sem("m_ld1")]
        km_done = sem("km_done"); exp_done = sem("exp_done"); p2_done = sem("p2_done")
        pv_done = sem("pv_done"); cn_ok = sem("cn_ok"); ct_done = sem("ct_done"); ct_evac = sem("ct_evac")
        op_done = sem("op_done"); xa_ok = sem("xa_ok")
        lg_done = sem("lg_done"); lg_evac = sem("lg_evac"); g_ok = sem("g_ok"); gt_done = sem("gt_done"); gt_evac = sem("gt_evac")
        h_done = sem("h_done"); h_act = sem("h_act"); gb_done = sem("gb_done"); hs_ok = sem("hs_ok")
        y_done = sem("y_done"); xf_ok = sem("xf_ok")
        xd_ok = sem("xd_ok"); xr_ok = sem("xr_ok"); xk_ok = sem("xk_ok")
        r_done = sem("r_done"); r_act = sem("r_act"); kk_done = sem("kk_done"); kr_ok = sem("kr_ok"); ks_ok = sem("ks_ok")
        vv_done = sem("vv_done"); y_ok = sem("y_ok"); xo_ok = sem("xo_ok"); o_out = sem("o_out")

        block = ctx.enter_context(nc.Block())

        def bseq(Bi):
            return Bi % B, Bi // GB, Bi % GB

        NB = LAYERS * B
        KVB = bank[6]
        QB = bank[7]
        FILL = B + 3
        KR = [(0, 1), (2, 3)]

        def prep_at(L, s):
            g, p = divmod(s + 5, GB)
            G = L * NG + g
            return (G, p) if g <= NG and G < LAYERS * NG else (None, None)

        def ffn_norm_at(s):
            g, r = divmod(s - 10, GB)
            return g if s >= 10 and r == 0 and g < NG - 1 else None

        def ffn_turn_at(s):
            return NG - 2 if s == B + 3 else ffn_norm_at(s) if s < B else None

        LN_ORDER = [(0, 0), (0, 1), (0, 2), (0, 3), (1, 0), (1, 1), (1, 2), (1, 3),
                    (2, 0), (2, 1), (2, 2), (2, 3), (3, 0), (3, 1), (3, 2), (3, 3)]

        def ln_no(phase, g):
            return LN_ORDER.index((phase, g))

        @block.sync
        def _(sp):
            def x_load(g):
                sp.dma_start(X[:, GB * g:GB * g + GB, :], x[GB * g:GB * g + GB, :, :].rearrange("b s d -> s b d")).then_inc(x_in[g], 16)

            x_load(0)
            sp.dma_start(IDF[:, :], ident).then_inc(w_in, 16)
            sp.dma_start(WT[:, 0:2 * 128], wts[:, 0:2 * 128]).then_inc(w_in, 16)
            sp.dma_start(CT[:, 0:GK], ctxT[:, 0:GK]).then_inc(c_in, 16)
            sp.dma_start(BC[:, :], bcols).then_inc(w_in, 16)
            sp.dma_start(NEG[:, :], negidh).then_inc(w_in, 16)
            sp.dma_start(WT[:, 2 * 128:4 * 128], wts[:, 2 * 128:4 * 128]).then_inc(w_in1, 16)
            sp.dma_start(MU8[:, :, :], mask.rearrange("b s k -> s b k")).then_inc(m_in, 16)
            sp.dma_start(CT[:, GK:], ctxT[:, GK:]).then_inc(c_in2, 16)
            sp.dma_start(GA[:, :], gates.broadcast_to([128, 5])).then_inc(w_in1, 16)
            sp.dma_start(BR[:, :, :], brows.broadcast_to([128, LAYERS, 128])).then_inc(w_in1, 16)
            sp.dma_start(IDH[:, :], identh).then_inc(w_in1, 16)
            x_load(1)
            for i in range(2):
                sp.dma_start(KS[i][STACK:ROWS, :, :, :], onesrows).then_inc(ones_in, 16)

            def later_loads():
                sp.dma_start(WT[:, 4 * 128:], wts[:, 4 * 128:]).then_inc(w_in2, 16)
                sp.dma_start(W2S[:, :], w2sh).then_inc(w_in2, 16)
                sp.dma_start(SEL[:, :], sel).then_inc(w_in2, 16)
                sp.dma_start(RANK[:, :, :], rank).then_inc(w_in2, 16)
                x_load(2)
                x_load(3)

            def k_store(G):
                sp.wait_ge(k_evac, PARTS * (G + 1))
                if G >= 2:
                    for f in range(2):
                        sp.wait_ge(k_ld[G % 2][f], 16 * PARTS * (G // 2))
                for p in range(PARTS):
                    sp.dma_start(kparts[G % 2, :, p].rearrange("f d h t -> (d h) f t"), kp[:, p, :].rearrange("r (f t) -> r f t", f=2)).then_inc(k_st, 16)

            def k_load(G, f):
                sp.wait_ge(k_st, 16 * PARTS * (G + 1))
                if G >= 2:
                    sp.wait_ge(km_done, (GB * (G - 2) + 2 * (f + 1)) * UNITS)
                src = kparts[G % 2, f].rearrange("c d h t -> (c d) h t")
                n = PARTS * HD
                for a in range(PARTS):
                    sp.dma_start(KS[G % 2][a * n:(a + 1) * n, f, :, :], src).then_inc(k_ld[G % 2][f], 16)

            def q_store(G):
                sp.wait_ge(q_evac, PARTS * (G + 1))
                if G >= 2:
                    for f in range(2):
                        sp.wait_ge(q_ld[G % 2][f], 16 * PARTS * (G // 2))
                for p in range(PARTS):
                    sp.dma_start(qparts[G % 2, :, p].rearrange("f d h t -> (d h) f t"), qp[:, p, :].rearrange("r (f t) -> r f t", f=2)).then_inc(q_st, 16)

            def q_load(G, f):
                sp.wait_ge(q_st, 16 * PARTS * (G + 1))
                if G >= 2:
                    sp.wait_ge(km_done, (GB * (G - 2) + 2 * (f + 1)) * UNITS)
                n = PARTS * HD
                for a in range(PARTS):
                    sp.dma_start(QS[G % 2][a * n:(a + 1) * n, f, :, :],
                                 qparts[G % 2, f, a].unsqueeze(0).broadcast_to([PARTS, HD, H, GT // 2])).then_inc(q_ld[G % 2][f], 16)

            def max_rows(Bi):
                b, G, k = bseq(Bi)
                sp.wait_ge(nt_evac, Bi + 1)
                if G >= 2 and k % 2 == 0:
                    sp.wait_ge(km_done, (GB * (G - 2) + k + 2) * UNITS)
                for p in range(PARTS):
                    sp.dma_start(QS[G % 2][STACK + p:STACK + p + 1, k // 2, :, (k % 2) * S:(k % 2 + 1) * S],
                                 nmT[Bi % 2][p * H:(p + 1) * H, :]).then_inc(m_ld[Bi % 2], 16)

            k_store(0)
            k_load(0, 0)
            q_store(0)
            q_load(0, 0)
            k_load(0, 1)
            q_load(0, 1)
            later_loads()
            for L in range(LAYERS):
                for s in range(B + 1):
                    if s >= 1:
                        max_rows(L * B + s - 1)
                    G, p = prep_at(L, s)
                    if G is not None and p == 1:
                        k_store(G)
                    if G is not None and p == 2:
                        k_load(G, 0)
                        if G != NG:
                            q_store(G)
                    if G is not None and p == 3:
                        if G != NG:
                            q_load(G, 0)
                        k_load(G, 1)
                        if G != NG:
                            q_load(G, 1)
                if L == 0:
                    q_store(NG)
                    q_load(NG, 0)
                    q_load(NG, 1)
            for g in range(NG):
                sp.wait_ge(xo_ok, g + 1)
                sp.dma_start(out[GB * g:GB * g + GB, :, :].rearrange("b s d -> s b d"), X[:, GB * g:GB * g + GB, :]).then_inc(o_out, 16)
            sp.wait_ge(o_out, 16 * NG)

        @block.gpsimd
        def _(po):
            po.memset(epsT[:, :], EPS).then_inc(pool_c, 1)
            po.memset(powT[:, :], -0.5).then_inc(pool_c, 1)
            for i in range(3):
                po.memset(VS[i][:, :, :, PARTS * HD:VC], 1.0).then_inc(pool_c, 1)
            po.memset(gx[:, :, :], 0.0).then_inc(pool_c, 1)
            po.memset(xsh[:, :, 0:1], 0.0).then_inc(pool_c, 1)
            po.wait_ge(pool_c, 7)
            po.memset(gx[:, :, HID + E:], 1.0).then_inc(pool_c, 1)

            def ln_rstd_(n):
                po.wait_ge(ln_var, n + 1)
                po.tensor_tensor(ve[:, :], mv[:, :, 1], epsT[:, :], ALU.add).then_inc(ln_rstd, 1)
                po.wait_ge(ln_rstd, 2 * n + 1)
                po.tensor_tensor(rstd[:, :], ve[:, :], powT[:, :], ALU.pow).then_inc(ln_rstd, 1)

            def bias_on_x(G):
                L, g = G // NG, G % NG
                po.wait_ge(xn_ok, ln_no(2 * L, g) + 1)
                po.wait_ge(bo_ok, L + 1)
                xg = X[:, GB * g:GB * g + GB, :]
                po.tensor_tensor(xg, xg, tgbo[:, L, :].unsqueeze(1).broadcast_to([S, GB, D]), ALU.add).then_inc(xb_ok, 1)

            def p_low(Bi, half):
                po.wait_ge(exp_done, Bi * UNITS + 2 * half + 2)
                if Bi >= 3:
                    po.wait_ge(pv_done, Bi - 2)
                hh = slice(8 * half, 8 * half + 8)
                po.tensor_tensor(P2[Bi % 3][:, hh, :], P32[Bi % 2][:, hh, :], P1[Bi % 3][:, hh, :], ALU.subtract).then_inc(p2_done, 1)

            def add_ffn_low(g):
                po.wait_ge(y_ok, g + 1)
                xg = X[:, GB * g:GB * g + GB, :]
                po.tensor_tensor(xg, xg, yv[g % 2], ALU.add).then_inc(xo_ok, 1)

            def x_difference(g):
                po.wait_ge(xt_evac, ln_no(3, g) + 1)
                if g >= 1:
                    po.wait_ge(xk_ok, g)
                po.tensor_tensor(xd, xsh[:, GB * g:GB * g + GB, 1:S + 1], xsh[:, GB * g:GB * g + GB, 0:S], ALU.subtract).then_inc(xd_ok, 1)

            ln_rstd_(ln_no(0, 0))
            for L in range(LAYERS):
                ln_rstd_(ln_no(2 * L, 1))
                for s in range(B + 6):
                    G, p = prep_at(L, s)
                    if 3 <= s < B + 3:
                        p_low(L * B + s - 3, 0)
                    if p == 0 and G != NG:
                        ln_rstd_(ln_no(2 * L, G % NG))
                    if s < B and ffn_norm_at(s) is not None:
                        ln_rstd_(ln_no(2 * L + 1, ffn_norm_at(s)))
                    if s < B and s % GB == 1:
                        bias_on_x(L * NG + s // GB)
                    if 3 <= s < B + 3:
                        p_low(L * B + s - 3, 1)
                    if s == B + 2:
                        ln_rstd_(ln_no(2 * L + 1, NG - 2))
                    if L == 1 and s in (FILL - 2, FILL - 1, FILL + 1):
                        x_difference((FILL - 2, FILL - 1, FILL + 1).index(s))
                ln_rstd_(ln_no(2 * L + 1, NG - 1))
                if L == 0:
                    ln_rstd_(ln_no(2, 0))
                else:
                    add_ffn_low(0)
                    add_ffn_low(1)
                    add_ffn_low(2)

        @block.vector
        def _(v):
            n_chain = [0]

            def mark(ins):
                n_chain[0] += 1
                ins.then_inc(dve_c, 1)
                return n_chain[0]

            def link(ins):
                v.wait_ge(dve_c, mark(ins))

            def ln(phase, g):
                n = ln_no(phase, g)
                if phase == 0:
                    v.wait_ge(x_in[g], 16)
                if phase in (1, 3):
                    v.wait_ge(xa_ok, B * (phase // 2) + GB * (g + 1))
                if phase == 2:
                    v.wait_ge(xf_ok, g + 1)
                if n >= 1:
                    v.wait_ge(ln_rstd, 2 * n)
                for i in range(GB):
                    nc.vector.bn_stats(st6[:, i, :], X[:, GB * g + i, :]).then_inc(dve_c, 1)
                n_chain[0] += GB
                v.wait_ge(dve_c, n_chain[0])
                for i in range(GB):
                    ins = nc.vector.bn_aggr(mv[:, i, :], st6[:, i, :])
                    if i < GB - 1:
                        ins.then_inc(dve_c, 1)
                n_chain[0] += GB - 1
                ins.then_inc(ln_var, 1)

            def ln_apply(phase, g):
                n = ln_no(phase, g)
                v.wait_ge(ln_rstd, 2 * n + 2)
                v.wait_ge(ln_var, n + 1)
                v.wait_ge(dve_c, n_chain[0])
                if n >= 1:
                    v.wait_ge(xt_done, n)
                for i in range(GB):
                    ins = nc.vector.tensor_scalar(xn[:, i, :], X[:, GB * g + i, :], mv[:, i, 0:1], rstd[:, i:i + 1],
                                                  ALU.subtract, ALU.mult)
                ins.then_inc(xn_ok, 1)

            def row_max(Bi, r):
                U = Bi * UNITS + r
                v.wait_ge(qm_done, U + 1)
                if r == 0 and Bi >= 2:
                    v.wait_ge(nm_ok, Bi - 1)
                ins = nc.vector.tensor_reduce(nmx[Bi % 2][:, UH * r:UH * r + UH],
                                              bank[U % 2][:, 0:UH * SK].rearrange("p (h k) -> p h k", k=SK),
                                              AX.X, ALU.max, negate=True)
                ins.then_inc(max_done, 1)

            def parts_and_normalise(Bi, Bn):
                a = Bi is not None
                c = Bn is not None
                if a:
                    i = Bi % 2
                    v.wait_ge(max_done, UNITS * (Bi + 1))
                    if Bi >= 1:
                        v.wait_ge(nm_ok, Bi)
                    if Bi >= 2:
                        v.wait_ge(nt_done, Bi - 1)
                    first = mark(nc.vector.tensor_copy(nmp[i][:, 0, :], nmx[i][:, :]))
                if c:
                    v.wait_ge(pv_done, Bn + 1)
                    if Bn >= 1:
                        v.wait_ge(cn_ok, Bn)
                    if Bn >= 2:
                        v.wait_ge(ct_done, Bn - 1)
                    pv = bank[4][:, 0:H * VC].rearrange("p (h c) -> p h c", c=VC)
                    mark(nc.vector.tensor_reduce(num[:, :, :], pv[:, :, 0:PARTS * HD].rearrange("p h (c d) -> p h d c", d=HD), AX.X, ALU.add))
                if a:
                    v.wait_ge(dve_c, first)
                    second = mark(nc.vector.tensor_tensor(nmr[:, :], nmx[i][:, :], nmp[i][:, 0, :], ALU.subtract))
                if c:
                    total = mark(nc.vector.reciprocal(rec[:, :], pv[:, :, PARTS * HD]))
                if a:
                    v.wait_ge(dve_c, second)
                    third = mark(nc.vector.tensor_copy(nmp[i][:, 1, :], nmr[:, :]))
                if c:
                    v.wait_ge(dve_c, total)
                    nc.vector.tensor_tensor(cn[Bn % 2][:, :].rearrange("p (h d) -> p h d", d=HD), num[:, :, :],
                                            rec[:, :].unsqueeze(2).broadcast_to([S, H, HD]), ALU.mult).then_inc(cn_ok, 1)
                if a:
                    v.wait_ge(dve_c, third)
                    nc.vector.tensor_tensor(nmp[i][:, 2, :], nmr[:, :], nmp[i][:, 1, :], ALU.subtract).then_inc(nm_ok, 1)

            def add_attention(Bi):
                b, G, k = bseq(Bi)
                v.wait_ge(op_done, Bi + 1)
                if k == 0:
                    v.wait_ge(xb_ok, G + 1)
                nc.vector.scalar_tensor_tensor(X[:, b, :], bank[5][:, 0:128], TG[:, 2 * (Bi // B):2 * (Bi // B) + 1],
                                               X[:, b, :], ALU.mult, ALU.add).then_inc(xa_ok, 1)

            def bias_row(L):
                v.wait_ge(bo_done, LAYERS)
                v.wait_ge(w_in1, 64)
                v.wait_ge(tg_ok, 1)
                link(nc.vector.tensor_tensor(tgbo[:, L, :], bank[4][:, 128 * L:128 * L + 128], BR[:, L, :], ALU.add))
                nc.vector.tensor_scalar(tgbo[:, L, :], tgbo[:, L, :], TG[:, 2 * L:2 * L + 1], None, ALU.mult).then_inc(bo_ok, 1)

            def last_k(G):
                v.wait_ge(k_done, PARTS * (G + 1))
                L = G // NG
                nc.vector.tensor_scalar(kp[:, PARTS - 1, :], KVB[:, 0:GK], BC[:, 2 * L + 1:2 * L + 2], None, ALU.add).then_inc(k_evac, 1)

            def last_q(G):
                v.wait_ge(q_done, PARTS * (G + 1))
                L = G // NG
                nc.vector.tensor_scalar(qp[:, PARTS - 1, :], QB[:, :], BC[:, 2 * L:2 * L + 1], None, ALU.add).then_inc(q_evac, 1)

            def last_v(G):
                v.wait_ge(v_done, PARTS * (G + 1))
                nc.vector.tensor_copy(VS[G % 3][:, :, :, 2 * HD:3 * HD],
                                      KVB[0:SK, :].rearrange("p (b h d) -> p b h d", h=H, d=HD)).then_inc(v_evac, 1)

            ln(0, 0)
            ln_apply(0, 0)
            v.wait_ge(w_in, 64)
            last_k(0)
            v.wait_ge(m_in, 16)
            nc.vector.tensor_scalar(MB[:, :, :], MU8[:, :, :], MASKED, None, ALU.mult).then_inc(mb_ok, 1)
            last_q(0)
            ln(0, 1)
            last_v(0)
            ln_apply(0, 1)

            def moe_top(lo, hi):
                v.wait_ge(lg_evac, hi // GB)
                if lo == 0:
                    v.wait_ge(w_in2, 64)
                c = sc[:, lo:hi, :]
                link(nc.vector.tensor_scalar(c, c, 1.0, None, ALU.add))
                link(nc.vector.reciprocal(c, c))
                link(nc.vector.tensor_scalar(c, c, GA[:, 4:5], None, ALU.mult))
                best(sc, m1, oh1, lo, hi)
                link(nc.vector.scalar_tensor_tensor(s2[:, lo:hi, :], oh1[:, lo:hi, :], -1e30, c, ALU.mult, ALU.add))

            def wide(x, lo, hi):
                return x[:, lo:hi].unsqueeze(2).broadcast_to([S, hi - lo, E])

            def best(src, m, oh, lo, hi):
                e = eq[:, lo:hi, :]
                link(nc.vector.tensor_reduce(m[:, lo:hi], src[:, lo:hi, :], AX.X, ALU.max))
                link(nc.vector.tensor_tensor(e, src[:, lo:hi, :], wide(m, lo, hi), ALU.is_equal))
                link(nc.vector.tensor_tensor(e, e, RANK[:, lo:hi, :], ALU.mult))
                link(nc.vector.tensor_reduce(mw[:, lo:hi], e, AX.X, ALU.max))
                link(nc.vector.tensor_tensor(oh[:, lo:hi, :], e, wide(mw, lo, hi), ALU.is_equal))

            def moe_gate(lo, hi):
                if lo == 0:
                    v.wait_ge(pool_c, 8)
                n = slice(lo, hi)
                best(s2, m2, oh2, lo, hi)
                link(nc.vector.tensor_tensor(den[:, n], m1[:, n], m2[:, n], ALU.add))
                link(nc.vector.reciprocal(den[:, n], den[:, n]))
                for m, oh in ((m1, oh1), (m2, oh2)):
                    link(nc.vector.tensor_tensor(m[:, n], m[:, n], den[:, n], ALU.mult))
                    link(nc.vector.tensor_tensor(oh[:, n, :], oh[:, n, :], wide(m, lo, hi), ALU.mult))
                gg = gx[:, n, HID:HID + E]
                link(nc.vector.tensor_tensor(gg, oh1[:, n, :], oh2[:, n, :], ALU.add))
                link(nc.vector.tensor_copy(gp[:, n, 0, :], gg))
                link(nc.vector.tensor_tensor(gr[:, n, :], gg, gp[:, n, 0, :], ALU.subtract))
                link(nc.vector.tensor_copy(gp[:, n, 1, :], gr[:, n, :]))
                nc.vector.tensor_tensor(gp[:, n, 2, :], gr[:, n, :], gp[:, n, 1, :], ALU.subtract).then_inc(g_ok, 1)

            def gate_hidden(g, k):
                i = g * NBLK + k
                v.wait_ge(gb_done, i + 1)
                v.wait_ge(h_act, g * (NBLK + 1) + k + 1)
                if g >= 1:
                    v.wait_ge(y_done, g)
                nc.vector.tensor_tensor(hs[:, k, :], bank[2 + i % 2][:, :], hT[:, k, :], ALU.mult).then_inc(hs_ok, 1)

            def add_moe(g):
                v.wait_ge(y_done, g + 1)
                xg = X[:, GB * g:GB * g + GB, :]
                nc.vector.scalar_tensor_tensor(xg, bank[4][:, :].rearrange("p (b d) -> p b d", d=D), TG[:, 1:2], xg,
                                               ALU.mult, ALU.add).then_inc(xf_ok, 1)

            def mix(g):
                if g < NG - 1:
                    v.wait_ge(xd_ok, g + 1)
                else:
                    v.wait_ge(xt_evac, ln_no(3, g) + 1)
                    link(nc.vector.tensor_tensor(xd, xsh[:, GB * g:GB * g + GB, 1:S + 1], xsh[:, GB * g:GB * g + GB, 0:S], ALU.subtract))
                for j, (o, w, ok) in enumerate(((xk, kk_done, xk_ok), (xr, r_done, xr_ok))):
                    if g >= 2:
                        v.wait_ge(w, g - 1)
                    nc.vector.scalar_tensor_tensor(o[g % 2], xd, BC[:, 10 - j:11 - j], xsh[:, GB * g:GB * g + GB, 0:S],
                                                   ALU.mult, ALU.add).then_inc(ok, 1)

            def k_square(g):
                v.wait_ge(kr_ok, g + 1)
                if g >= 1:
                    v.wait_ge(vv_done, g)
                k = bank[KR[g % 2][0]][:, :]
                nc.vector.scalar_tensor_tensor(ksq, k, 0.0, kre, ALU.max, ALU.mult).then_inc(ks_ok, 1)

            def add_ffn(g):
                v.wait_ge(vv_done, g + 1)
                v.wait_ge(r_act, g + 1)
                if g >= 2:
                    v.wait_ge(xo_ok, g - 1)
                nc.vector.scalar_tensor_tensor(yv[g % 2], bank[KR[g % 2][1]][:, :].rearrange("p (b d) -> p b d", d=D),
                                                    TG[:, 3:4], rs, ALU.mult, ALU.mult).then_inc(y_ok, 1)
                if g == NG - 1:
                    v.wait_ge(y_ok, g + 1)
                    v.wait_ge(xo_ok, g)
                    xg = X[:, GB * g:GB * g + GB, :]
                    nc.vector.tensor_tensor(xg, xg, yv[g % 2], ALU.add).then_inc(xo_ok, 1)

            for L in range(LAYERS):
                for s in range(B + 6):
                    G, p = prep_at(L, s)
                    norm = None
                    if p == 0 and G != NG:
                        norm = (2 * L, G % NG)
                    if ffn_norm_at(s) is not None:
                        norm = (2 * L + 1, ffn_norm_at(s))
                    for r in range(UNITS):
                        u = UNITS * p + r if G is not None else None
                        if u == K_STEPS[2] + 1:
                            last_k(G)
                        if u == Q_STEPS[2] + 1 and G != NG:
                            last_q(G)
                        if u == V_STEPS[2] + 1:
                            last_v(G)
                        if s < B:
                            row_max(L * B + s, r)
                        if norm and r == 0:
                            ln(*norm)
                        if r == 0 and s >= 6:
                            add_attention(L * B + s - 6)
                        if r == 2 and 4 <= s < B + 4:
                            parts_and_normalise(None, L * B + s - 4)
                        if norm and r == 1 and s < B:
                            ln_apply(*norm)
                    if s < B:
                        parts_and_normalise(L * B + s, None)
                    if s == B + 2:
                        ln_apply(2 * L + 1, NG - 2)
                    if L == 0 and s == 1:
                        bias_row(0)
                        bias_row(1)
                    if L == 0 and s == B:
                        moe_top(0, B // 2)
                    if L == 0 and s == B + 1:
                        moe_gate(0, B // 2)
                    if L == 1 and s in (FILL - 2, FILL - 1):
                        mix(s - FILL + 2)
                    if L == 1 and s == FILL:
                        k_square(0)
                        mix(NG - 2)
                    if L == 1 and s == FILL + 1:
                        add_ffn(0)
                        k_square(1)
                    if L == 1 and s == 0:
                        add_moe(NG - 1)
                ln(2 * L + 1, NG - 1)
                if L == 0:
                    gate_hidden(0, 0)
                    gate_hidden(0, 1)
                    ln_apply(1, NG - 1)
                    for g in range(NG - 1):
                        for k in range(NBLK):
                            if g > 0 or k > 1:
                                gate_hidden(g, k)
                        if g == 0:
                            moe_top(B // 2, B)
                        if g >= 1:
                            add_moe(g - 1)
                        if g == 1:
                            moe_gate(B // 2, B)
                            ln(2, 0)
                            ln_apply(2, 0)
                        if g == 2:
                            last_q(NG)
                            ln(2, 1)
                            ln_apply(2, 1)
                    add_moe(NG - 2)
                    for k in range(NBLK):
                        gate_hidden(NG - 1, k)
                else:
                    ln_apply(3, NG - 1)
                    add_ffn(1)
                    k_square(2)
                    mix(NG - 1)
                    add_ffn(2)
                    k_square(NG - 1)
                    add_ffn(NG - 1)

        @block.scalar
        def _(a):
            a.wait_ge(w_in, 64)

            def xt_copy(phase, g):
                n = ln_no(phase, g)
                a.wait_ge(xt_done, n + 1)
                src = (KVB if phase == 3 or phase == 1 and g < NG - 1 else QB)[:, :]
                if phase == 1:
                    nc.scalar.activation(XT4[:, g, :], src, ACT.Copy).then_inc(xt_evac, 1)
                elif phase == 3:
                    nc.scalar.activation(xsh[:, GB * g:GB * g + GB, 1:S + 1], src.rearrange("p (b s) -> p b s", s=S), ACT.Copy).then_inc(xt_evac, 1)
                else:
                    nc.scalar.activation(xnT[:, :], src, ACT.Copy).then_inc(xt_evac, 1)

            def q_part(G, p):
                a.wait_ge(q_done, PARTS * G + p + 1)
                if G >= 1 and p == 0:
                    a.wait_ge(q_st, 16 * PARTS * G)
                L = G // NG
                nc.scalar.activation(qp[:, p, :], QB[:, :], ACT.Identity, bias=BC[:, 2 * L:2 * L + 1]).then_inc(q_evac, 1)

            def k_part(G, p):
                a.wait_ge(k_done, PARTS * G + p + 1)
                if G >= 1 and p == 0:
                    a.wait_ge(k_st, 16 * PARTS * G)
                L = G // NG
                nc.scalar.activation(kp[:, p, :], KVB[:, 0:GK], ACT.Identity, bias=BC[:, 2 * L + 1:2 * L + 2]).then_inc(k_evac, 1)

            def v_part(G, p):
                a.wait_ge(v_done, PARTS * G + p + 1)
                if G >= 3 and p == 0:
                    a.wait_ge(pv_done, GB * (G - 2))
                nc.scalar.activation(VS[G % 3][:, :, :, p * HD:(p + 1) * HD],
                                     KVB[0:SK, :].rearrange("p (b h d) -> p b h d", h=H, d=HD), ACT.Copy).then_inc(v_evac, 1)

            def nt_copy(Bi):
                a.wait_ge(nt_done, Bi + 1)
                if Bi >= 2:
                    a.wait_ge(m_ld[Bi % 2], 48 * (Bi // 2))
                nc.scalar.activation(nmT[Bi % 2][:, :], bank[5][:, :].bitcast(BF16)[0:PARTS * H, 0:S], ACT.Copy).then_inc(nt_evac, 1)

            def exps(Bi, r):
                U = Bi * UNITS + r
                i = Bi % 2
                a.wait_ge(km_done, U + 1)
                if r == 0 and Bi >= 2:
                    a.wait_ge(p2_done, 2 * (Bi - 1))
                if r == 0 and Bi >= 3:
                    a.wait_ge(pv_done, Bi - 2)
                hh = slice(UH * r, UH * r + UH)
                src = bank[2 + U % 2][0:SK, :].rearrange("p (h s) -> p h s", s=S)
                nc.scalar.activation(P32[i][:, hh, :], src, ACT.Exp, bias=LIFT, scale=SCALE)
                nc.scalar.activation(P1[Bi % 3][:, hh, :], src, ACT.Exp, bias=LIFT, scale=SCALE).then_inc(exp_done, 1)

            def ct_copy(Bi):
                a.wait_ge(ct_done, Bi + 1)
                if Bi >= 2:
                    a.wait_ge(op_done, Bi - 1)
                nc.scalar.activation(cT[Bi % 2][:, :], bank[5][:, 0:128], ACT.Copy).then_inc(ct_evac, 1)

            def prep(G, u):
                for p in range(PARTS - 1):
                    if u == K_STEPS[p] + 1:
                        k_part(G, p)
                    if u == Q_STEPS[p] + 1 and G != NG:
                        q_part(G, p)
                    if u == V_STEPS[p] + 1:
                        v_part(G, p)
                if u == TURN_STEP + 1 and G != NG:
                    xt_copy(2 * (G // NG), G % NG)

            k_part(0, 0)
            xt_copy(0, 0)
            k_part(0, 1)
            for p in range(PARTS - 1):
                q_part(0, p)
            for p in range(PARTS - 1):
                v_part(0, p)
            a.wait_ge(w_in1, 64)
            nc.scalar.activation(TG[:, :], GA[:, 0:4], ACT.Tanh).then_inc(tg_ok, 1)

            def logit_exp(g):
                a.wait_ge(lg_done, g + 1)
                nc.scalar.activation(sc[:, GB * g:GB * g + GB, :], (KVB if g < NG - 1 else QB)[:, 0:GB * E].rearrange("p (b e) -> p b e", e=E),
                                     ACT.Exp, scale=-1.0).then_inc(lg_evac, 1)

            def gt_copy(g):
                a.wait_ge(gt_done, g + 1)
                nc.scalar.activation(gpT[:, :], bank[5][:, :].bitcast(BF16)[0:PARTS * E, 512:1024], ACT.Copy)
                if g >= 2:
                    a.wait_ge(y_done, g - 1)
                nc.scalar.activation(h5[g % 2][HID:HID + E + 1, :], bank[6][HID:HID + E + 1, :], ACT.Copy).then_inc(gt_evac, 1)

            def gelu(g, k):
                j = g * (NBLK + 1) + k
                a.wait_ge(h_done, j + 1)
                if k < NBLK:
                    i = g * NBLK + k
                    if i >= NBLK:
                        a.wait_ge(hs_ok, i - NBLK + 1)
                    nc.scalar.activation(hT[:, k, :], bank[j % 2][:, :], ACT.Gelu, bias=BC[:, 4 + k:5 + k]).then_inc(h_act, 1)
                else:
                    if g >= 2:
                        a.wait_ge(y_done, g - 1)
                    nc.scalar.activation(h5[g % 2][0:HID, :], bank[j % 2][0:HID, :], ACT.Gelu, bias=BC[0:HID, 8:9]).then_inc(h_act, 1)

            def k_relu(g):
                a.wait_ge(kk_done, g + 1)
                if g >= 1:
                    a.wait_ge(ks_ok, g)
                nc.scalar.activation(kre, bank[KR[g % 2][0]][:, :], ACT.Relu).then_inc(kr_ok, 1)

            def r_sig(g):
                a.wait_ge(r_done, g + 1)
                if g >= 1:
                    a.wait_ge(y_ok, g)
                nc.scalar.activation(rs, QB[:, :].rearrange("p (b d) -> p b d", d=D), ACT.Sigmoid).then_inc(r_act, 1)

            for L in range(LAYERS):
                for u in range(UNITS):
                    prep(L * NG + 1, u)
                for s in range(B + 6):
                    G, p = prep_at(L, s)
                    for r in range(UNITS):
                        if G is not None:
                            prep(G, UNITS * p + r)
                        if r == (2 if s > 1 else 0) and 1 <= s < B + 1:
                            nt_copy(L * B + s - 1)
                        if r == 0 and 6 <= s:
                            ct_copy(L * B + s - 6)
                        U = UNITS * s + r - LAG
                        if 0 <= U < B * UNITS:
                            exps(L * B + U // UNITS, U % UNITS)
                        if r == 3 and ffn_turn_at(s) is not None:
                            xt_copy(2 * L + 1, ffn_turn_at(s))
                        if L == 0 and r == 0 and ffn_turn_at(s - 1) is not None:
                            logit_exp(ffn_turn_at(s - 1))
                    if L == 0 and s > FILL:
                        gelu(0, s - FILL - 1)
                    if L == 1 and s in (FILL - 1, FILL):
                        k_relu(s - FILL + 1)
                    if L == 1 and s in (FILL - 1, FILL + 1):
                        r_sig((s - FILL + 1) // 2)
                if L == 0:
                    gt_copy(0)
                    for k in range(2, NBLK + 1):
                        gelu(0, k)
                    for g in range(NG):
                        if g + 1 < NG:
                            for k in range(NBLK + 1):
                                gelu(g + 1, k)
                                if g == 0 and k == 2:
                                    xt_copy(1, NG - 1)
                                if g == 2 and k == 1:
                                    xt_copy(2, 0)
                                if g == 2 and k in (2, 3):
                                    q_part(NG, k - 2)
                        if g == 0:
                            logit_exp(NG - 1)
                        if g + 1 < NG:
                            gt_copy(g + 1)
                else:
                    k_relu(NG - 2)
                    xt_copy(3, NG - 1)
                    r_sig(NG - 2)
                    k_relu(NG - 1)
                    r_sig(NG - 1)

        @block.tensor
        def _(pe):
            mm = nc.tensor.matmul

            kv_reader = [None]
            q_reader = [None]

            def bank_read(reader):
                if reader[0]:
                    pe.wait_ge(*reader[0])

            def k_proj(G, p):
                L, g = G // NG, G % NG
                if p == 0:
                    bank_read(kv_reader)
                    mm(KVB[:, 0:GK], W(WK[L]), CT[:, g * GK:(g + 1) * GK], start=True, stop=True).then_inc(k_done, 1)
                    kv_reader[0] = (k_evac, PARTS * (G + 1))
                else:
                    pe.wait_ge(k_evac, PARTS * G + p)
                    mm(KVB[:, 0:GK], NEG[:, :], kp[:, p - 1, :], start=False, stop=True, skip_group_check=True).then_inc(k_done, 1)

            def turn(phase, g):
                n = ln_no(phase, g)
                o, reader = (KVB, kv_reader) if phase == 3 or phase == 1 and g < NG - 1 else (QB, q_reader)
                bank_read(reader)
                pe.wait_ge(xn_ok, n + 1)
                for i in range(GB):
                    last = nc.tensor.transpose(o[:, i * S:(i + 1) * S], xn[:, i, :], IDF[:, :])
                last.then_inc(xt_done, 1)
                reader[0] = (xt_evac, n + 1)

            def q_proj(G, p):
                L, g = G // NG, G % NG
                if p == 0:
                    bank_read(q_reader)
                    mm(QB[:, :], W(WQ[L]), xnT[:, :], start=True, stop=True).then_inc(q_done, 1)
                    q_reader[0] = (q_evac, PARTS * (G + 1))
                else:
                    pe.wait_ge(q_evac, PARTS * G + p)
                    mm(QB[:, :], NEG[:, :], qp[:, p - 1, :], start=False, stop=True, skip_group_check=True).then_inc(q_done, 1)

            def v_proj(G, p):
                L, g = G // NG, G % NG
                if p == 0:
                    bank_read(kv_reader)
                    for i in range(GB):
                        c = (g * GB + i) * SK
                        last = mm(KVB[0:SK, i * D:(i + 1) * D], CT[:, c:c + SK], W(WV[L]), start=(i == 0), stop=True, skip_group_check=True)
                    last.then_inc(v_done, 1)
                    kv_reader[0] = (v_evac, PARTS * (G + 1))
                else:
                    pe.wait_ge(v_evac, PARTS * G + p)
                    mm(KVB[0:SK, :].rearrange("p (b h d) -> p b h d", h=H, d=HD), NEG[0:SK, 0:SK],
                       VS[G % 3][:, :, :, (p - 1) * HD:p * HD], start=False, stop=True, skip_group_check=True).then_inc(v_done, 1)

            def bias_product(L):
                mm(bank[4][:, 128 * L:128 * L + 128], BC[:, 11 + L:12 + L].broadcast_to([128, 128]), W(WO[L]), start=True, stop=True).then_inc(bo_done, 1)

            def scores_q(Bi, r):
                b, G, k = bseq(Bi)
                U = Bi * UNITS + r
                o = bank[U % 2]
                if U >= 2:
                    pe.wait_ge(max_done, U - 1)
                if r == 0 and k % 2 == 0:
                    pe.wait_ge(q_ld[G % 2][k // 2], 16 * PARTS * (G // 2 + 1))
                    pe.wait_ge(k_ld[G % 2][k // 2], 16 * PARTS * (G // 2 + 1))
                masked = Bi < B
                if masked:
                    mm(o[:, 0:UH * SK].rearrange("p (h k) -> p h k", k=SK), IDH[:, :],
                       MB[:, b, :].unsqueeze(1).broadcast_to([S, UH, SK]), start=True, stop=False, skip_group_check=True)
                for j in range(UH):
                    h = UH * r + j
                    last = mm(o[:, j * SK:(j + 1) * SK], QS[G % 2][0:STACK, k // 2, h, (k % 2) * S:(k % 2 + 1) * S],
                              KS[G % 2][0:STACK, k // 2, h, (k % 2) * SK:(k % 2 + 1) * SK], start=not masked, stop=True, skip_group_check=True)
                last.then_inc(qm_done, 1)

            def scores_k(Bi, r):
                b, G, k = bseq(Bi)
                U = Bi * UNITS + r
                o = bank[2 + U % 2]
                if U >= 2:
                    pe.wait_ge(exp_done, U - 1)
                if r == 0:
                    pe.wait_ge(m_ld[Bi % 2], 48 * (Bi // 2 + 1))
                masked = Bi < B
                if masked:
                    mm(o[0:SK, :].rearrange("p (h s) -> p h s", s=S), MB[:, b, :],
                       IDH[:, :].unsqueeze(1).broadcast_to([S, UH, S]), start=True, stop=False, skip_group_check=True)
                for j in range(UH):
                    h = UH * r + j
                    last = mm(o[0:SK, j * S:(j + 1) * S], KS[G % 2][0:ROWS, k // 2, h, (k % 2) * SK:(k % 2 + 1) * SK],
                              QS[G % 2][0:ROWS, k // 2, h, (k % 2) * S:(k % 2 + 1) * S], start=not masked, stop=True, skip_group_check=True)
                last.then_inc(km_done, 1)

            def turn_max(Bi):
                pe.wait_ge(nm_ok, Bi + 1)
                if Bi >= 1:
                    pe.wait_ge(nt_evac, Bi)
                if Bi % B >= 5:
                    pe.wait_ge(xa_ok, Bi - 4)
                elif Bi >= B:
                    pe.wait_ge(xa_ok, B)
                nc.tensor.transpose(bank[5][:, :].bitcast(BF16)[0:PARTS * H, 0:S],
                                    nmp[Bi % 2][:, :, :].rearrange("p c h -> p (c h)"), IDH[:, :]).then_inc(nt_done, 1)

            def values(Bi, half):
                b, G, k = bseq(Bi)
                if half == 1:
                    pe.wait_ge(p2_done, 2 * (Bi + 1))
                    for h in range(H // 2, H):
                        last = value_head(Bi, h)
                    last.then_inc(pv_done, 1)
                    return
                pe.wait_ge(p2_done, 2 * Bi + 1)
                if Bi >= 1:
                    pe.wait_ge(cn_ok, Bi)
                if Bi == 0:
                    pe.wait_ge(bo_ok, LAYERS)
                if k == 0:
                    pe.wait_ge(v_evac, PARTS * (G + 1))
                for h in range(H // 2):
                    value_head(Bi, h)

            def value_head(Bi, h):
                b, G, k = bseq(Bi)
                o = bank[4][:, h * VC:(h + 1) * VC]
                mm(o, P1[Bi % 3][:, h, :], VS[G % 3][:, k, h, :], start=(h == 0), stop=False, skip_group_check=True)
                return mm(o, P2[Bi % 3][:, h, :], VS[G % 3][:, k, h, :], start=False, stop=True, skip_group_check=True)

            def turn_ctx(Bi):
                pe.wait_ge(cn_ok, Bi + 1)
                pe.wait_ge(nt_evac, min(Bi + 5, B * (Bi // B + 1)))
                if Bi % B >= 1:
                    pe.wait_ge(xa_ok, Bi)
                nc.tensor.transpose(bank[5][:, 0:128], cn[Bi % 2][:, :], IDF[:, :]).then_inc(ct_done, 1)

            def out_proj(Bi):
                pe.wait_ge(ct_evac, Bi + 1)
                mm(bank[5][:, 0:128], cT[Bi % 2][:, :], W(WO[Bi // B]), start=True, stop=True).then_inc(op_done, 1)

            def prep(G, u):
                if u in K_STEPS:
                    k_proj(G, K_STEPS.index(u))
                if u == TURN_STEP and G != NG:
                    turn(2 * (G // NG), G % NG)
                if u in Q_STEPS and G != NG:
                    q_proj(G, Q_STEPS.index(u))
                if u in V_STEPS:
                    v_proj(G, V_STEPS.index(u))

            def hidden(g, k):
                j = g * (NBLK + 1) + k
                if j >= 2:
                    pe.wait_ge(h_act, j - 1)
                if k < NBLK:
                    mm(bank[j % 2][:, :], W(W1 + k), XT4[:, g, :], start=True, stop=True).then_inc(h_done, 1)
                else:
                    mm(bank[j % 2][0:HID, :], W(WSH, HID), XT4[:, g, :], start=True, stop=True).then_inc(h_done, 1)

            def turn_gates(g):
                pe.wait_ge(g_ok, g // 2 + 1)
                if g >= 1:
                    pe.wait_ge(gt_evac, g)
                else:
                    pe.wait_ge(xa_ok, B)
                    bank_read(kv_reader)
                for i in range(GB):
                    nc.tensor.transpose(bank[5][:, :].bitcast(BF16)[0:PARTS * E, 512 + i * S:512 + (i + 1) * S],
                                        gp[:, GB * g + i, :, :].rearrange("p c e -> p (c e)"), IDH[:, :])
                for i in range(GB):
                    last = nc.tensor.transpose(bank[6][0:HID + E + 1, i * S:(i + 1) * S], gx[:, GB * g + i, :], IDF[:, :])
                last.then_inc(gt_done, 1)

            def logits(g):
                o, reader = (KVB, kv_reader) if g < NG - 1 else (QB, q_reader)
                bank_read(reader)
                for i in range(GB):
                    last = mm(o[:, i * E:(i + 1) * E], XT4[:, g, i * S:(i + 1) * S], W(WGATE, E), start=True, stop=True)
                last.then_inc(lg_done, 1)
                reader[0] = (lg_evac, g + 1)

            def gate_rows(g, k):
                i = g * NBLK + k
                if k == 0:
                    pe.wait_ge(gt_evac, g + 1)
                if i >= 2:
                    pe.wait_ge(hs_ok, i - 1)
                mm(bank[2 + i % 2][:, :], SEL[:, k * 128:(k + 1) * 128], gpT[:, :], start=True, stop=True).then_inc(gb_done, 1)

            def moe_out(g, i):
                if i == 0:
                    pe.wait_ge(hs_ok, (g + 1) * NBLK)
                    pe.wait_ge(h_act, (g + 1) * (NBLK + 1))
                    if g == 0:
                        pe.wait_ge(cn_ok, B)
                    else:
                        pe.wait_ge(xf_ok, g)
                for k in range(NBLK + 1):
                    lhs = hs[:, k, i * S:(i + 1) * S] if k < NBLK else h5[g % 2][:, i * S:(i + 1) * S]
                    rhs = W(W2 + k) if k < NBLK else W2S[:, :]
                    last = mm(bank[4][:, i * D:(i + 1) * D], lhs, rhs, start=(k == 0), stop=(k == NBLK))
                if i == GB - 1:
                    last.then_inc(y_done, 1)

            def kr_mix(g):
                pe.wait_ge(xk_ok, g + 1)
                if g == 0:
                    pe.wait_ge(max_done, NB * UNITS)
                if g == 1:
                    pe.wait_ge(exp_done, NB * UNITS)
                if g >= 2:
                    pe.wait_ge(ks_ok, g - 1)
                mm(bank[KR[g % 2][0]][:, :], W(WKK), xk[g % 2].rearrange("p b s -> p (b s)"), start=True, stop=True).then_inc(kk_done, 1)
                pe.wait_ge(xr_ok, g + 1)
                if g >= 1:
                    pe.wait_ge(r_act, g)
                for i in range(GB):
                    last = mm(QB[:, i * D:(i + 1) * D], xr[g % 2][:, i, :], W(WR), start=True, stop=True)
                last.then_inc(r_done, 1)
                q_reader[0] = (r_act, g + 1)

            def v_mix(g):
                pe.wait_ge(ks_ok, g + 1)
                if g >= 2:
                    pe.wait_ge(y_ok, g - 1)
                for i in range(GB):
                    last = mm(bank[KR[g % 2][1]][:, i * D:(i + 1) * D], ksq[:, i * S:(i + 1) * S], W(WVV), start=True, stop=True)
                last.then_inc(vv_done, 1)

            pe.wait_ge(w_in, 64)
            pe.wait_ge(c_in, 16)
            k_proj(0, 0)
            turn(0, 0)
            k_proj(0, 1)
            q_proj(0, 0)
            k_proj(0, 2)
            q_proj(0, 1)
            q_proj(0, 2)
            pe.wait_ge(w_in1, 64)
            for p in range(PARTS):
                v_proj(0, p)
            pe.wait_ge(c_in2, 16)
            pe.wait_ge(pool_c, 8)
            pe.wait_ge(mb_ok, 1)
            pe.wait_ge(ones_in, 32)

            for L in range(LAYERS):
                for u in range(UNITS):
                    prep(L * NG + 1, u)
                for s in range(B + 6):
                    G, p = prep_at(L, s)
                    for r in range(UNITS):
                        if s < B:
                            scores_q(L * B + s, r)
                        if r == (2 if s > 1 else 0) and 1 <= s < B + 1:
                            turn_max(L * B + s - 1)
                        U = UNITS * s + r - LAG
                        if 0 <= U < B * UNITS:
                            scores_k(L * B + U // UNITS, U % UNITS)
                        if r == 1 and 6 <= s:
                            out_proj(L * B + s - 6)
                        if r in VALUE_STEPS and 4 <= s < B + 4:
                            values(L * B + s - 4, VALUE_STEPS.index(r))
                        if r == 3 and 5 <= s < B + 5:
                            turn_ctx(L * B + s - 5)
                        if G is not None:
                            prep(G, UNITS * p + r)
                        if r == 3 and ffn_turn_at(s) is not None:
                            turn(2 * L + 1, ffn_turn_at(s))
                        if L == 0 and r == 0 and ffn_turn_at(s - 1) is not None:
                            logits(ffn_turn_at(s - 1))
                        if L == 1 and s == 0:
                            moe_out(NG - 1, r)
                    if L == 0 and s == 1:
                        pe.wait_ge(w_in2, 64)
                        bias_product(0)
                        bias_product(1)
                    if L == 0 and s == B + 1:
                        pe.wait_ge(max_done, B * UNITS)
                        hidden(0, 0)
                        hidden(0, 1)
                    if L == 1 and s == FILL - 1:
                        kr_mix(0)
                    if L == 1 and s == FILL:
                        kr_mix(1)
                        v_mix(0)
                if L == 0:
                    pe.wait_ge(exp_done, B * UNITS)
                    turn_gates(0)
                    for k in range(2, NBLK + 1):
                        hidden(0, k)
                    for g in range(NG - 1):
                        for k in range(NBLK + 1):
                            if k < NBLK and (g, k) != (2, 0):
                                gate_rows(g, k)
                            hidden(g + 1, k)
                            if (g, k) == (2, 0):
                                gate_rows(g, k)
                            if g == 0 and k == 2:
                                turn(1, NG - 1)
                            if g == 2 and k == 1:
                                turn(2, 0)
                            if g == 2 and k >= 2:
                                q_proj(NG, k - 2)
                        if g == 0:
                            logits(NG - 1)
                        if g in (0, 2):
                            turn_gates(g + 1)
                        if g < NG - 1:
                            for i in range(GB):
                                moe_out(g, i)
                        if g == 1:
                            turn_gates(g + 1)
                    for k in range(NBLK):
                        gate_rows(NG - 1, k)
                    pe.wait_ge(h_act, NG * (NBLK + 1))
                    kv_reader[0] = (gt_evac, NG)
                else:
                    v_mix(1)
                    kr_mix(2)
                    turn(3, NG - 1)
                    v_mix(2)
                    kr_mix(NG - 1)
                    v_mix(NG - 1)


def kernel(**inputs):
    import numpy as np
    import ml_dtypes
    import concourse.bacc as bacc
    from concourse import mybir as mb
    from concourse.bass_utils import run_bass_kernel_spmd as run

    a = {k: np.asarray(v) for k, v in inputs.items()}
    f = np.float32

    def pad(w):
        o = np.zeros((128, 128), f)
        o[:w.shape[0], :w.shape[1]] = w
        return o

    w1 = a["L0_ffn_W1"].transpose(1, 0, 2).reshape(D, E * HID)
    w2 = a["L0_ffn_W2"].reshape(E * HID, D)
    def by_feature(w):
        return w.reshape(*w.shape[:-1], H, HD).swapaxes(-1, -2).reshape(w.shape)

    blocks = [by_feature(a["L0_xattn_Wq"]), by_feature(a["L0_xattn_Wk"]), a["L0_xattn_Wv"], a["L0_xattn_Wo"],
              by_feature(a["L1_xattn_Wq"].T), by_feature(a["L1_xattn_Wk"].T), a["L1_xattn_Wv"].T, a["L1_xattn_Wo"].T]
    blocks += [w1[:, 128 * i:128 * i + 128] for i in range(NBLK)]
    blocks += [pad(a["L0_ffn_Ws1"]), pad(a["L0_ffn_gate_W"])]
    blocks += [w2[128 * i:128 * i + 128, :] for i in range(NBLK)]
    blocks += [a["L1_ffn_W_r"].T, a["L1_ffn_W_k"].T, a["L1_ffn_W_v"].T]
    b1 = a["L0_ffn_b1"].reshape(NBLK, 128)
    bs1 = np.zeros(128, f)
    bs1[:HID] = a["L0_ffn_bs1"]
    cols = [*(by_feature(a[f"L{i}_xattn_b{x}"]) for i in range(LAYERS) for x in "qk"), *b1, bs1,
            a["L1_ffn_mu_r"], a["L1_ffn_mu_k"], a["L0_xattn_bv"], a["L1_xattn_bv"]]
    sel = np.zeros((PARTS, E, NBLK, 2, HID), ml_dtypes.bfloat16)
    for e in range(E):
        sel[:, e, e // 2, e % 2, :] = 1
    arrays = {
        "x": a["x"],
        "ctxT": a["ctx_1024"].reshape(B * SK, D).T,
        "mask": a["mask_Bx1xSxS2_bk1"].reshape(B, S, SK),
        "wts": np.concatenate(blocks, axis=1),
        "w2sh": np.concatenate([a["L0_ffn_Ws2"], a["L0_ffn_b2"], a["L0_ffn_bs2"][None]], axis=0),
        "bcols": np.stack(cols, axis=1),
        "brows": np.stack([a["L0_xattn_bo"], a["L1_xattn_bo"]])[None],
        "gates": np.stack([a["g_xattn"][0], a["g_ffn"][0], a["g_xattn"][1], a["g_ffn"][1],
                           a["L0_ffn_route_scale"].reshape(())])[None],
        "ident": np.eye(128, dtype=f),
        "identh": np.eye(128, dtype=f).astype(ml_dtypes.bfloat16),
        "negidh": -np.eye(128, dtype=f).astype(ml_dtypes.bfloat16),
        "sel": sel.reshape(PARTS * E, NBLK * 128),
        "rank": np.broadcast_to(np.arange(E, 0, -1, dtype=f), (128, B, E)),
        "onesrows": np.ones((PARTS, 2, H, GK // 2), ml_dtypes.bfloat16),
    }
    nc = bacc.Bacc("TRN2", target_bir_lowering=False, num_devices=1)
    named, args = {}, []
    for name, v in arrays.items():
        v = np.ascontiguousarray(v)
        named[f"in_{name}"] = v
        args.append(nc.dram_tensor(f"in_{name}", v.shape, mb.dt.from_np(v.dtype), kind="ExternalInput").ap())
    out = nc.dram_tensor("out_0", (B, S, D), mb.dt.float32, kind="ExternalOutput").ap()
    gated_blocks(nc, *args, out)
    r = run(nc, [named], core_ids=[0])
    return r.results[0]["out_0"]
```
